# Optimizing a Trainium2 kernel written in Bass

```python
import numpy as np
import jax
import jax.numpy as jnp

def _softmax(x, axis=-1):
    return jax.nn.softmax(x, axis=axis)

def _gelu(x):
    return jax.nn.gelu(x, approximate=True)

def _silu(x):
    return jax.nn.silu(x)

def _sigmoid(x):
    return jax.nn.sigmoid(x)

def _layernorm(x, axis=-1, eps=1e-05):
    m = jnp.mean(x, axis=axis, keepdims=True)
    v = jnp.var(x, axis=axis, keepdims=True)
    return (x - m) / jnp.sqrt(v + eps)

def _scatter_add(tgt, idx, src, axis=0):
    return tgt.at[idx].add(src)

def _segment_sum(src, seg, n):
    return jax.ops.segment_sum(src, seg, n)
kernel_name = 'mk_flamingo_gated_d1_seqx_r8_384460'

def setup_inputs(seed: int=0):
    np.random.seed(seed)
    _w = jnp.asarray

    def _rec_inputs():
        import jax
        import jax.numpy as jnp
        _rk = jax.random.key(seed)
        x = 7.22e-05 + 1 * jax.random.normal(jax.random.fold_in(_rk, 1), (4, 512, 128), jnp.float32)
        _lenS = 512 - jax.random.randint(jax.random.fold_in(_rk, 7), (4,), 0, max(1, 512 // 4) + 1, jnp.int32)
        _lenS2 = 32 - jax.random.randint(jax.random.fold_in(_rk, 8), (4,), 0, max(1, 32 // 4) + 1, jnp.int32)
        _ctx_1024P = jax.random.normal(jax.random.fold_in(_rk, 11), (4, 16, 128), jnp.float32)
        _ctx_1024c = jax.random.dirichlet(jax.random.fold_in(_rk, 511), 0.3 * jnp.ones((16,), jnp.float32), (4, 32))
        _ctx_1024t = jnp.einsum('bsk,bkd->bsd', _ctx_1024c, _ctx_1024P)
        _ctx_1024t = _ctx_1024t * jax.lax.rsqrt(jnp.mean(jnp.square(_ctx_1024t)) + 1e-12) * 0.953939
        ctx_1024 = 4.13588e-05 + 0.999923 * (_ctx_1024t + 0.3 * jax.random.normal(jax.random.fold_in(_rk, 611), (4, 32, 128), jnp.float32))
        _g = jax.random.normal(jax.random.fold_in(_rk, 9001), (2, 1), jnp.float32)
        _g = jnp.sign(_g) * jnp.maximum(jnp.abs(_g), 1.0) + (_g == 0) * 1.0
        g_xattn = _g[0]
        g_ffn = _g[1]
        return (x, ctx_1024, g_xattn, g_ffn)
    x, ctx_1024, g_xattn, g_ffn = _rec_inputs()

    def _L0_xattn_setup():
        import jax, jax.numpy as jnp
        import numpy as np
        B, SQ, SK, D = (4, 256, 256, 128)
        key = jax.random.key(seed)
        ks = jax.random.split(key, 8)
        s = 1.0 / np.sqrt(D)
        return {'input_seq': jax.random.normal(ks[0], (B, SQ, D), jnp.float32), 'condition_seq': jax.random.normal(ks[1], (B, SK, D), jnp.float32), 'Wq': jax.random.normal(ks[2], (D, D), jnp.float32) * s, 'bq': jnp.zeros((D,), jnp.float32), 'Wk': jax.random.normal(ks[3], (D, D), jnp.float32) * s, 'bk': jnp.zeros((D,), jnp.float32), 'Wv': jax.random.normal(ks[4], (D, D), jnp.float32) * s, 'bv': jnp.zeros((D,), jnp.float32)}
    _L0_xattn_all = _L0_xattn_setup()
    _L0_xattn_in = {k: v for k, v in _L0_xattn_all.items() if k in ('Wq', 'bq', 'Wk', 'bk', 'Wv', 'bv')}
    del _L0_xattn_all

    def _L0_ffn_setup():
        import jax, jax.numpy as jnp
        import numpy as np
        DIM = 128
        DEPTH = 6
        HEADS = 16
        DIM_HEAD = 64
        WINDOW = 32
        INNER = HEADS * DIM_HEAD
        DIM_INNER = int(DIM * 4 * 2 / 3)
        QK_SCALE = 8.0

        def shift_tokens(t):
            a, s = jnp.split(t, 2, -1)
            s = jnp.pad(s, ((0, 0), (1, 0), (0, 0)))[:, :-1]
            return jnp.concatenate([a, s], -1)

        def l2norm(t):
            return t / jnp.maximum(jnp.linalg.norm(t, axis=-1, keepdims=True), 1e-12)

        def rotate_half(x):
            x1, x2 = jnp.split(x, 2, -1)
            return jnp.concatenate([-x2, x1], -1)

        def rotary_tables(n):
            half = jnp.arange(0, DIM_HEAD, 2, dtype=jnp.float32)
            inv_freq = 1.0 / 10000.0 ** (half / DIM_HEAD)
            t = jnp.arange(n, dtype=jnp.float32)
            freqs = t[:, None] * inv_freq[None, :]
            freqs = jnp.concatenate([freqs, freqs], -1)
            base_scale = (half + 0.4 * DIM_HEAD) / (1.4 * DIM_HEAD)
            power = (t - n // 2) / (WINDOW // 2)
            scale = base_scale[None, :] ** power[:, None]
            scale = jnp.concatenate([scale, scale], -1)
            return (freqs, scale)

        def local_attention(q, k, v):
            b, h, n, d = q.shape
            w = WINDOW
            nw = n // w
            bq = q.reshape(b, h, nw, w, d)
            bk = k.reshape(b, h, nw, w, d)
            bv = v.reshape(b, h, nw, w, d)

            def look(t):
                p = jnp.pad(t, ((0, 0), (0, 0), (1, 0), (0, 0), (0, 0)))
                return jnp.concatenate([p[:, :, :nw], p[:, :, 1:]], axis=3)
            bk2, bv2 = (look(bk), look(bv))
            seq = jnp.arange(n).reshape(nw, w)
            seq_p = jnp.pad(seq, ((1, 0), (0, 0)), constant_values=-1)
            jt = jnp.concatenate([seq_p[:nw], seq_p[1:]], axis=1)
            it = seq[:, :, None]
            jb = jt[:, None, :]
            mask = (it < jb) | (it > jb + w) | (jb == -1)
            sim = jnp.einsum('bhwie,bhwje->bhwij', bq, bk2) * QK_SCALE
            sim = jnp.where(mask, -jnp.finfo(sim.dtype).max, sim)
            attn = jax.nn.softmax(sim, -1)
            out = jnp.einsum('bhwij,bhwje->bhwie', attn, bv2)
            return out.reshape(b, h, n, d)

        def attn_layer(x, Wqkv, qs, ksc, Wo):
            b, n, _ = x.shape
            qkv = x @ Wqkv
            q, k, v = jnp.split(qkv, 3, -1)
            sh = lambda t: t.reshape(b, n, HEADS, DIM_HEAD).transpose(0, 2, 1, 3)
            q, k, v = (sh(q), sh(k), sh(v))
            q = l2norm(q) * qs
            k = l2norm(k) * ksc
            freqs, scale = rotary_tables(n)
            cos, sin = (jnp.cos(freqs), jnp.sin(freqs))
            q = q * cos * scale + rotate_half(q) * sin * scale
            inv = 1.0 / scale
            k = k * cos * inv + rotate_half(k) * sin * inv
            out = local_attention(q, k, v)
            out = out.transpose(0, 2, 1, 3).reshape(b, n, INNER)
            return out @ Wo

        def ffn_layer(x, g, bln, W1, b1, W2, b2):
            mu = x.mean(-1, keepdims=True)
            var = ((x - mu) ** 2).mean(-1, keepdims=True)
            xn = (x - mu) / jnp.sqrt(var + 1e-05) * g + bln
            hg = xn @ W1 + b1
            a, gate = jnp.split(hg, 2, -1)
            return a * jax.nn.gelu(gate, approximate=False) @ W2 + b2
        key = jax.random.key(seed)
        ks = jax.random.split(key, 8)
        B, N = (2, 256)
        init = lambda k, shape: jax.random.normal(k, shape, jnp.float32) * 0.02
        return {'x': jax.random.normal(ks[0], (B, N, DIM), jnp.float32), 'Wqkv': init(ks[1], (DEPTH, DIM, 3 * INNER)), 'q_scale': jnp.ones((DEPTH, DIM_HEAD), jnp.float32), 'k_scale': jnp.ones((DEPTH, DIM_HEAD), jnp.float32), 'Wo': init(ks[2], (DEPTH, INNER, DIM)), 'ln_g': jnp.ones((DEPTH, DIM), jnp.float32), 'ln_b': jnp.zeros((DEPTH, DIM), jnp.float32), 'W1': init(ks[3], (DEPTH, DIM, 2 * DIM_INNER)), 'b1': jnp.zeros((DEPTH, 2 * DIM_INNER), jnp.float32), 'W2': init(ks[4], (DEPTH, DIM_INNER, DIM)), 'b2': jnp.zeros((DEPTH, DIM), jnp.float32)}
    _L0_ffn_all = _L0_ffn_setup()
    _L0_ffn_in = {k: v for k, v in _L0_ffn_all.items() if k in ('Wqkv', 'q_scale', 'k_scale', 'Wo', 'ln_g', 'ln_b', 'W1', 'b1', 'W2', 'b2')}
    del _L0_ffn_all
    return {'x': x, 'ctx_1024': ctx_1024, 'g_xattn': g_xattn, 'g_ffn': g_ffn, 'L0_xattn_Wq': _L0_xattn_in['Wq'], 'L0_xattn_bq': _L0_xattn_in['bq'], 'L0_xattn_Wk': _L0_xattn_in['Wk'], 'L0_xattn_bk': _L0_xattn_in['bk'], 'L0_xattn_Wv': _L0_xattn_in['Wv'], 'L0_xattn_bv': _L0_xattn_in['bv'], 'L0_ffn_Wqkv': _L0_ffn_in['Wqkv'], 'L0_ffn_q_scale': _L0_ffn_in['q_scale'], 'L0_ffn_k_scale': _L0_ffn_in['k_scale'], 'L0_ffn_Wo': _L0_ffn_in['Wo'], 'L0_ffn_ln_g': _L0_ffn_in['ln_g'], 'L0_ffn_ln_b': _L0_ffn_in['ln_b'], 'L0_ffn_W1': _L0_ffn_in['W1'], 'L0_ffn_b1': _L0_ffn_in['b1'], 'L0_ffn_W2': _L0_ffn_in['W2'], 'L0_ffn_b2': _L0_ffn_in['b2']}

def reference(x, ctx_1024, g_xattn, g_ffn, L0_xattn_Wq, L0_xattn_bq, L0_xattn_Wk, L0_xattn_bk, L0_xattn_Wv, L0_xattn_bv, L0_ffn_Wqkv, L0_ffn_q_scale, L0_ffn_k_scale, L0_ffn_Wo, L0_ffn_ln_g, L0_ffn_ln_b, L0_ffn_W1, L0_ffn_b1, L0_ffn_W2, L0_ffn_b2):
    import jax
    import jax.numpy as jnp

    def _L0_xattn_ref(input_seq, condition_seq, Wq, bq, Wk, bk, Wv, bv):
        import jax, jax.numpy as jnp
        import numpy as np
        B, SQ, SK, D = (4, 256, 256, 128)
        q = jnp.einsum('bsd,ed->bse', input_seq, Wq) + bq
        k = jnp.einsum('btd,ed->bte', condition_seq, Wk) + bk
        v = jnp.einsum('btd,ed->bte', condition_seq, Wv) + bv
        scores = jnp.einsum('bse,bte->bst', q, k)
        attn = jax.nn.softmax(scores, axis=-1)
        attended = jnp.einsum('bst,bte->bse', attn, v)
        return attended

    def _L0_ffn_ref(x, Wqkv, q_scale, k_scale, Wo, ln_g, ln_b, W1, b1, W2, b2):
        import jax, jax.numpy as jnp
        import numpy as np
        DIM = 128
        DEPTH = 6
        HEADS = 16
        DIM_HEAD = 64
        WINDOW = 32
        INNER = HEADS * DIM_HEAD
        DIM_INNER = int(DIM * 4 * 2 / 3)
        QK_SCALE = 8.0

        def shift_tokens(t):
            a, s = jnp.split(t, 2, -1)
            s = jnp.pad(s, ((0, 0), (1, 0), (0, 0)))[:, :-1]
            return jnp.concatenate([a, s], -1)

        def l2norm(t):
            return t / jnp.maximum(jnp.linalg.norm(t, axis=-1, keepdims=True), 1e-12)

        def rotate_half(x):
            x1, x2 = jnp.split(x, 2, -1)
            return jnp.concatenate([-x2, x1], -1)

        def rotary_tables(n):
            half = jnp.arange(0, DIM_HEAD, 2, dtype=jnp.float32)
            inv_freq = 1.0 / 10000.0 ** (half / DIM_HEAD)
            t = jnp.arange(n, dtype=jnp.float32)
            freqs = t[:, None] * inv_freq[None, :]
            freqs = jnp.concatenate([freqs, freqs], -1)
            base_scale = (half + 0.4 * DIM_HEAD) / (1.4 * DIM_HEAD)
            power = (t - n // 2) / (WINDOW // 2)
            scale = base_scale[None, :] ** power[:, None]
            scale = jnp.concatenate([scale, scale], -1)
            return (freqs, scale)

        def local_attention(q, k, v):
            b, h, n, d = q.shape
            w = WINDOW
            nw = n // w
            bq = q.reshape(b, h, nw, w, d)
            bk = k.reshape(b, h, nw, w, d)
            bv = v.reshape(b, h, nw, w, d)

            def look(t):
                p = jnp.pad(t, ((0, 0), (0, 0), (1, 0), (0, 0), (0, 0)))
                return jnp.concatenate([p[:, :, :nw], p[:, :, 1:]], axis=3)
            bk2, bv2 = (look(bk), look(bv))
            seq = jnp.arange(n).reshape(nw, w)
            seq_p = jnp.pad(seq, ((1, 0), (0, 0)), constant_values=-1)
            jt = jnp.concatenate([seq_p[:nw], seq_p[1:]], axis=1)
            it = seq[:, :, None]
            jb = jt[:, None, :]
            mask = (it < jb) | (it > jb + w) | (jb == -1)
            sim = jnp.einsum('bhwie,bhwje->bhwij', bq, bk2) * QK_SCALE
            sim = jnp.where(mask, -jnp.finfo(sim.dtype).max, sim)
            attn = jax.nn.softmax(sim, -1)
            out = jnp.einsum('bhwij,bhwje->bhwie', attn, bv2)
            return out.reshape(b, h, n, d)

        def attn_layer(x, Wqkv, qs, ksc, Wo):
            b, n, _ = x.shape
            qkv = x @ Wqkv
            q, k, v = jnp.split(qkv, 3, -1)
            sh = lambda t: t.reshape(b, n, HEADS, DIM_HEAD).transpose(0, 2, 1, 3)
            q, k, v = (sh(q), sh(k), sh(v))
            q = l2norm(q) * qs
            k = l2norm(k) * ksc
            freqs, scale = rotary_tables(n)
            cos, sin = (jnp.cos(freqs), jnp.sin(freqs))
            q = q * cos * scale + rotate_half(q) * sin * scale
            inv = 1.0 / scale
            k = k * cos * inv + rotate_half(k) * sin * inv
            out = local_attention(q, k, v)
            out = out.transpose(0, 2, 1, 3).reshape(b, n, INNER)
            return out @ Wo

        def ffn_layer(x, g, bln, W1, b1, W2, b2):
            mu = x.mean(-1, keepdims=True)
            var = ((x - mu) ** 2).mean(-1, keepdims=True)
            xn = (x - mu) / jnp.sqrt(var + 1e-05) * g + bln
            hg = xn @ W1 + b1
            a, gate = jnp.split(hg, 2, -1)
            return a * jax.nn.gelu(gate, approximate=False) @ W2 + b2
        for i in range(DEPTH):
            x = attn_layer(shift_tokens(x), Wqkv[i], q_scale[i], k_scale[i], Wo[i]) + x
            x = ffn_layer(shift_tokens(x), ln_g[i], ln_b[i], W1[i], b1[i], W2[i], b2[i]) + x
        return x
    x = x + jnp.tanh(g_xattn[0]) * _L0_xattn_ref(_layernorm(x, axis=-1), ctx_1024, L0_xattn_Wq, L0_xattn_bq, L0_xattn_Wk, L0_xattn_bk, L0_xattn_Wv, L0_xattn_bv)
    x = x + jnp.tanh(g_ffn[0]) * _L0_ffn_ref(_layernorm(x, axis=-1), L0_ffn_Wqkv, L0_ffn_q_scale, L0_ffn_k_scale, L0_ffn_Wo, L0_ffn_ln_g, L0_ffn_ln_b, L0_ffn_W1, L0_ffn_b1, L0_ffn_W2, L0_ffn_b2)
    return x

_drawn_inputs = setup_inputs


def setup_inputs(seed=0):
    import zlib

    import numpy as np

    out = dict(_drawn_inputs(seed))
    spreads = {'L0_xattn_bq': (0.0, 0.1),
     'L0_xattn_bk': (0.0, 0.8),
     'L0_xattn_bv': (0.0, 0.1),
     'L0_ffn_q_scale': (1.0, 0.6),
     'L0_ffn_k_scale': (1.0, 0.6),
     'L0_ffn_ln_g': (1.0, 0.6),
     'L0_ffn_ln_b': (0.0, 0.8),
     'L0_ffn_b1': (0.0, 0.1),
     'L0_ffn_b2': (0.0, 0.1)}
    factors = {}
    for name, (base, spread) in spreads.items():
        noise = np.random.default_rng([zlib.crc32(name.encode()), seed]).standard_normal(out[name].shape)
        drawn = base * np.exp(spread * noise) if base else spread * noise
        out[name] = jnp.asarray(drawn.astype(out[name].dtype))
    for name, factor in factors.items():
        out[name] = (out[name] * factor).astype(out[name].dtype)
    return out
```

```python
from contextlib import ExitStack

import concourse.bass as bass
from concourse import mybir

ALU = mybir.AluOpType
ACT = mybir.ActivationFunctionType
AX = mybir.AxisListType
F32 = mybir.dt.float32
BF16 = mybir.dt.bfloat16

P = 128
WIN = 32
QW = P // WIN
UN = 4


class Pos:

    def __init__(self, g, u):
        self.g, self.u = g, u

    def back(self, lag):
        d = (lag - self.u + UN - 1) // UN if lag > self.u else 0
        if isinstance(self.g, int) and self.g - d < 0:
            return None
        return Pos(self.g - d if d else self.g, self.u - lag + UN * d)

    def count(self, per, k):
        return self.g * (UN * per) + (self.u * per + k) if not isinstance(self.g, int) \
            else (self.g * UN + self.u) * per + k


def build(nc, x, ctx_in, g_xattn, g_ffn, Wq, bq, Wk, bk, Wv, bv, Wqkv, q_scale, k_scale, Wo, ln_g, ln_b,
          W1, b1, W2, b2, rope, masks, ident_in, out):
    B, N, D = x.shape
    NS = ctx_in.shape[1]
    L = Wqkv.shape[0]
    INNER = Wo.shape[1]
    DH = q_scale.shape[1]
    H = INNER // DH
    HP = H // 2
    HALF = DH // 2
    FI = W2.shape[1]
    FC = [(c, min(P, FI - c)) for c in range(0, FI, P)]
    NT = B * N // P
    G = L * B
    assert N == UN * P and D == P and B * NS == P and H * DH == 2 * 512 and NS == WIN
    NREST = 4 + len(FC)
    GL = 2

    with ExitStack() as ctx:
        def sb(name, shape, dt=F32):
            return ctx.enter_context(nc.sbuf_tensor(name, shape, dt))

        def bank(name):
            return ctx.enter_context(nc.psum_tensor(name, [P, 512], F32))

        def sem(name):
            return ctx.enter_context(nc.semaphore(name))

        X = [bank("px0"), bank("px1")]
        S = [bank("ps0"), bank("ps1")]
        O = [bank("po0"), bank("po1")]
        M = [bank("pm0"), bank("pm1")]

        wqkv = sb("wqkv", [P, 2, 3 * INNER])
        wo = sb("wo", [P, 2, HP, D])
        w1 = sb("w1", [P, 2, 2 * FI])
        w2 = sb("w2", [P, 2, len(FC), D])
        b1b = sb("b1b", [P, 2, 2 * FI])
        b2b = sb("b2b", [P, 2, D])
        lng = sb("lng", [P, L])
        lnb = sb("lnb", [P, L])
        tab = sb("tab", [P, L, UN, 4, DH])
        maskb = sb("maskb", [P, 2, HP, 2 * WIN], BF16)
        ident = sb("ident", [P, P])
        identb = sb("identb", [P, P], BF16)
        mhalf = sb("mhalf", [P, 2 * H])
        y = sb("y", [P, NT, D])
        x1 = sb("x1", [P, NT, D])
        xst = sb("xst", [P, B, N + 1])
        xstage = sb("xstage", [P, 2, P])
        qk = sb("qk", [P, 2, 2 * INNER])
        vb = sb("vb", [P, UN, INNER])
        t1 = sb("t1", [P, 2 * INNER])
        t2 = sb("t2", [P, 2 * INNER])
        qkr = sb("qkr", [P, 2 * INNER])
        ss = sb("ss", [P, 2, 2 * H])
        rn = sb("rn", [P, 2, 2 * H])
        qT = sb("qT", [P, 2, HP, P])
        kT = sb("kT", [P, 2, HP, WIN + P])
        smax = sb("smax", [P, H])
        ex = sb("ex", [P, H, 2 * WIN])
        ssum = sb("ssum", [P, H])
        rsum = sb("rsum", [P, H])
        pn = sb("pn", [P, H, 2 * WIN])
        pT = sb("pT", [P, 2, H, 2 * WIN])
        oT = sb("oT", [P, HP, P])
        y1s = sb("y1s", [P, D])
        y1b = sb("y1b", [P, D])
        y2s = sb("y2s", [P, D])
        fT = sb("fT", [P, N + 1])
        st = sb("st", [P, 6])
        mv = sb("mv", [P, 2])
        ve = sb("ve", [P, 1])
        rstd = sb("rstd", [P, 1])
        xn = sb("xn", [P, D])
        xnT = sb("xnT", [P, P])
        ha = sb("ha", [P, FI])
        hg = sb("hg", [P, FI])
        hu = sb("hu", [P, FI])
        uT = sb("uT", [P, len(FC), P])
        gates = sb("gates", [P, 2])
        tgate = sb("tgate", [P, 2])
        st16 = sb("st16", [P, NT, 6])
        mv16 = sb("mv16", [P, NT, 2])
        ve16 = sb("ve16", [P, NT])
        rs16 = sb("rs16", [P, NT])
        bqk = sb("bqk", [P, 2])
        sq = t2
        ropeb = pn[:, :, :].rearrange("p h j -> p (h j)").rearrange("p (u k d) -> p u k d", u=UN, k=4)
        qks = oT[:, 0:2 * L * DH // P, :].rearrange("p h t -> p (h t)").rearrange("p (a l d) -> p a l d", a=2, l=L)
        maskf = oT[:, HP - 1, :].rearrange("p (m j) -> p m j", m=2)
        xn16 = t1[:, :].rearrange("p (t d) -> p t d", d=D)
        xnT16 = t2[:, :]
        qTx = qkr[:, :]
        wx = qk[:, 0, 0:3 * P].rearrange("p (a d) -> p a d", a=3)
        cx = qk[:, 0, 3 * P:4 * P]
        wxT = qk[:, 0, 4 * P:8 * P]
        kTx = qk[:, 0, 8 * P:9 * P]
        vx = qk[:, 0, 9 * P:10 * P]
        bvb = qk[:, 0, 10 * P:11 * P]
        ex0 = qk[:, 1, 0:512]
        px = qk[:, 1, 512:1024]
        pxT = qk[:, 1, 1024:1536]

        x_in = [sem(f"x_in{b}") for b in range(B)]
        xw_in, const_in, rope_in = sem("xw_in"), sem("const_in"), sem("rope_in")
        wqkv_in, wrest_in = sem("wqkv_in"), sem("wrest_in")
        stored = sem("stored")
        const_set, zero_set, tab_set = sem("const_set"), sem("zero_set"), sem("tab_set")
        xs_stat, xs_aggr, xs_ve, xs_rstd, xs_norm = (sem(n) for n in
                                                     ("xs_stat", "xs_aggr", "xs_ve", "xs_rstd", "xs_norm"))
        xw_turned, xw_copied, xkv, xk_set, xv_set = (sem(n) for n in
                                                     ("xw_turned", "xw_copied", "xkv", "xk_set", "xv_set"))
        xn_turned, xn_copied, xq, xq_set, xsc = (sem(n) for n in ("xn_turned", "xn_copied", "xq", "xq_set", "xsc"))
        xmax, xsub, xexp, xsum, xrec, xp = (sem(n) for n in ("xmax", "xsub", "xexp", "xsum", "xrec", "xp"))
        xp_turned, xp_copied, xatt, gate_set, x1_set = (sem(n) for n in
                                                        ("xp_turned", "xp_copied", "xatt", "gate_set", "x1_set"))
        y0_turned, y0_copied = sem("y0_turned"), sem("y0_copied")
        staged = sem("staged")
        proj = sem("proj")
        proj_copied = sem("proj_copied")
        squared = sem("squared")
        ss_set = sem("ss_set")
        rn_set = sem("rn_set")
        roped = sem("roped")
        rope_sum = sem("rope_sum")
        qkr_set = sem("qkr_set")
        turned = sem("turned")
        turned_copied = sem("turned_copied")
        scored = sem("scored")
        max_set = sem("max_set")
        less_max = sem("less_max")
        exp_set = sem("exp_set")
        sum_set = sem("sum_set")
        rsum_set = sem("rsum_set")
        p_set = sem("p_set")
        pT_set = sem("pT_set")
        edge_done = sem("edge_done")
        win_done = sem("win_done")
        weighed = sem("weighed")
        oT_set = sem("oT_set")
        wo_done = sem("wo_done")
        y1_set = sem("y1_set")
        y1b_set = sem("y1b_set")
        y1_turned = sem("y1_turned")
        fT_set = sem("fT_set")
        f_back = sem("f_back")
        st_set, mv_set, ve_set = sem("st_set"), sem("mv_set"), sem("ve_set")
        rstd_set = sem("rstd_set")
        xn_set = sem("xn_set")
        xn_back = sem("xn_back")
        xnT_set = sem("xnT_set")
        h_done = sem("h_done")
        hb_set = sem("hb_set")
        gelu_set = sem("gelu_set")
        hu_set = sem("hu_set")
        u_turned = sem("u_turned")
        uT_set = sem("uT_set")
        w2_done = sem("w2_done")
        y2_set = sem("y2_set")
        y_kept = sem("y_kept")
        y2_turned = sem("y2_turned")
        xst_set = sem("xst_set")

        def wait(eng, s, at, per, k):
            if at is not None:
                eng.wait_ge(s, at.count(per, k))

        def layer(at):
            return at.g // B

        def row(at):
            return at.g % B

        def run(eng, step):
            for g in range(GL):
                for u in range(UN):
                    step(Pos(g, u), True)
            with eng.Fori(GL, G) as g:
                for u in range(UN):
                    step(Pos(g, u), True)
            for u in range(3):
                step(Pos(G, u), False)

        def lagged(at, lag):
            p = at.back(lag)
            return p if p is None or not isinstance(p.g, int) or p.g < G else None

        block = ctx.enter_context(nc.Block())

        @block.sync
        def _(sp):
            sp.dma_start(ident[:, :], ident_in).then_inc(const_in, 16)
            for b in range(B):
                sp.dma_start(x1[:, b * UN:(b + 1) * UN, :],
                             x[b].rearrange("(t p) d -> p t d", p=P)).then_inc(x_in[b], 16)
            for a, w in enumerate((Wq, Wk, Wv)):
                sp.dma_start(wx[:, a, :], w).then_inc(xw_in, 16)
            sp.dma_start(cx, ctx_in.rearrange("b s d -> (b s) d")).then_inc(xw_in, 16)
            sp.dma_start(bvb, bv.partition_broadcast(P)).then_inc(xw_in, 16)
            sp.dma_start(bqk[:, 0:1], bq.unsqueeze(1)).then_inc(xw_in, 16)
            sp.dma_start(bqk[:, 1:2], bk.unsqueeze(1)).then_inc(xw_in, 16)
            sp.dma_start(gates[:, 0:1], g_xattn.partition_broadcast(P)).then_inc(xw_in, 16)
            sp.dma_start(gates[:, 1:2], g_ffn.partition_broadcast(P)).then_inc(xw_in, 16)
            sp.dma_start(maskf[:, :, :], masks).then_inc(const_in, 16)
            sp.dma_start(ropeb[:, :, :, :], rope).then_inc(rope_in, 16)
            sp.dma_start(qks[:, 0, :, :], q_scale.partition_broadcast(P)).then_inc(rope_in, 16)
            sp.dma_start(qks[:, 1, :, :], k_scale.partition_broadcast(P)).then_inc(rope_in, 16)
            sp.dma_start(lng[:, :], ln_g).then_inc(rope_in, 16)
            sp.dma_start(lnb[:, :], ln_b).then_inc(rope_in, 16)

            for l in range(L):
                h = l % 2
                if l >= 1:
                    sp.wait_ge(wqkv_in, 16 * l)
                    sp.wait_ge(wrest_in, 16 * NREST * l)
                if l >= 2:
                    sp.wait_ge(y2_set, NT * (l - 1))
                sp.dma_start(wqkv[:, h, :], Wqkv[l]).then_inc(wqkv_in, 16)
                sp.dma_start(wo[:, h, :, :], Wo[l].rearrange("(h p) d -> p h d", p=P)).then_inc(wrest_in, 16)
                sp.dma_start(w1[:, h, :], W1[l]).then_inc(wrest_in, 16)
                for c, (f0, fn) in enumerate(FC):
                    sp.dma_start(w2[0:fn, h, c, :], W2[l, f0:f0 + fn, :]).then_inc(wrest_in, 16)
                sp.dma_start(b1b[:, h, :], b1[l].partition_broadcast(P)).then_inc(wrest_in, 16)
                sp.dma_start(b2b[:, h, :], b2[l].partition_broadcast(P)).then_inc(wrest_in, 16)
            for b in range(B):
                sp.wait_ge(x1_set, B + b + 1)
                sp.dma_start(out[b].rearrange("(t p) d -> p t d", p=P),
                             x1[:, b * UN:(b + 1) * UN, :]).then_inc(stored, 16)
            sp.wait_ge(stored, 16 * B)

        @block.scalar
        def _(act):
            act.wait_ge(xw_in, 16 * 9)
            act.activation(tgate[:, :], gates[:, :], ACT.Tanh).then_inc(gate_set, 1)
            act.wait_ge(xw_turned, 1)
            act.copy(wxT, M[0][:, :]).then_inc(xw_copied, 1)
            act.wait_ge(xkv, 1)
            act.activation(kTx, M[1][:, 0:P], ACT.Identity, bias=bqk[:, 1:2]).then_inc(xk_set, 1)
            for b in range(B):
                act.wait_ge(xn_turned, b + 1)
                act.copy(xnT16[:, b * N:(b + 1) * N], (X + O)[b][:, :]).then_inc(xn_copied, 1)
            for b in range(B):
                act.wait_ge(xq, b + 1)
                act.activation(qTx[:, b * N:(b + 1) * N], (X + O)[b][:, :], ACT.Identity,
                               bias=bqk[:, 0:1]).then_inc(xq_set, 1)
            act.wait_ge(xsub, 1)
            act.activation(ex0, ex0, ACT.Exp).then_inc(xexp, 1)
            act.wait_ge(xp_turned, 1)
            act.copy(pxT, M[0][:, :]).then_inc(xp_copied, 1)
            act.wait_ge(zero_set, 4)
            for b in range(B):
                act.wait_ge(y0_turned, b + 1)
                act.copy(xst[0:64, b, 0:N], (X + O)[b][0:64, :]).then_inc(y0_copied, 1)
                act.copy(xst[64:P, b, 1:N + 1], (X + O)[b][64:P, :]).then_inc(y0_copied, 1)
            act.wait_ge(y0_copied, 2)
            act.copy(xstage[:, 0, :], xst[:, 0, 0:P]).then_inc(staged, 1)

            def step(at, live):
                p, t, f = (at if live else None), lagged(at, 1), lagged(at, 3)
                par = at.u % 2
                tp = (at.u - 1) % 2
                c0 = P * f.u if f else 0

                def copy_weighed(n):
                    wait(act, weighed, f, 2, n + 1)
                    wait(act, wo_done, f.back(1), 1, 1)
                    act.copy(oT[:, 4 * n:4 * n + 4, :],
                             O[n][:, :].rearrange("p (h t) -> p h t", h=4)).then_inc(oT_set, 1)

                def copy_turned(n):
                    wait(act, turned, t, 4, n + 1)
                    if n == 0:
                        wait(act, scored, t.back(2), 2, 2)
                    src = X[n % 2][:, :].rearrange("p (h t) -> p h t", h=4)
                    dst = (qT[:, tp, 4 * n:4 * n + 4, :] if n < 2
                           else kT[:, tp, 4 * n - 8:4 * n - 4, WIN:WIN + P])
                    act.copy(dst, src).then_inc(turned_copied, 1)

                def carry_keys():
                    wait(act, turned_copied, t, 5, 4)
                    wait(act, scored, t.back(1), 2, 2)
                    act.copy(kT[:, 1 - tp, :, 0:WIN], kT[:, tp, :, P:P + WIN]).then_inc(turned_copied, 1)

                def shift_y1():
                    wait(act, y1_turned, f, 1, 1)
                    act.copy(fT[0:64, c0:c0 + P], M[1][0:64, 0:P]).then_inc(fT_set, 1)
                    act.copy(fT[64:P, c0 + 1:c0 + 1 + P], M[1][64:P, 0:P]).then_inc(fT_set, 1)

                def copy_proj(c):
                    wait(act, proj, p, 6, c + 1)
                    if c == 0:
                        wait(act, roped, p.back(2), 3, 3)
                    if c == 4:
                        wait(act, weighed, p.back(3), 2, 2)
                    dst = qk[:, par, c * 512:(c + 1) * 512] if c < 4 else vb[:, at.u, (c - 4) * 512:(c - 3) * 512]
                    act.copy(dst, X[c % 2][:, :]).then_inc(proj_copied, 1)

                def square(n):
                    wait(act, proj_copied, p, 6, 2 * n + 2)
                    if n == 0:
                        wait(act, rope_sum, p.back(1), 2, 2)
                    act.activation(sq[:, n * INNER:(n + 1) * INNER], qk[:, par, n * INNER:(n + 1) * INNER],
                                   ACT.Square).then_inc(squared, 1)

                def scale_xn():
                    l = layer(f)
                    act.wait_ge(rope_in, 16 * 5)
                    wait(act, xn_back, f, 1, 1)
                    act.activation(xnT[:, :], M[1][:, 0:P], ACT.Identity, scale=lng[:, bass.ds(l, 1)],
                                   bias=lnb[:, bass.ds(l, 1)]).then_inc(xnT_set, 1)

                def gelu():
                    wait(act, hb_set, f, 2, 1)
                    act.activation(hg[:, :], hg[:, :], ACT.Gelu).then_inc(gelu_set, 1)

                def copy_u():
                    wait(act, u_turned, f, 1, 1)
                    nf = len(FC) - 1
                    act.copy(uT[:, 0:nf, :], M[0][:, 0:nf * P].rearrange("p (c t) -> p c t", c=nf)).then_inc(uT_set, 1)
                    act.copy(uT[0:FC[nf][1], nf, :], M[0][0:FC[nf][1], nf * P:(nf + 1) * P]).then_inc(uT_set, 1)

                def exps():
                    wait(act, less_max, t, 2, 2)
                    act.activation(ex[:, :, :], ex[:, :, :], ACT.Exp).then_inc(exp_set, 1)

                def shift_y2():
                    wait(act, y2_turned, f, 1, 1)
                    r = row(f)
                    act.copy(xst[0:64, bass.ds(r, 1), c0:c0 + P].squeeze(1), M[0][0:64, 0:P]).then_inc(xst_set, 1)
                    act.copy(xst[64:P, bass.ds(r, 1), c0 + 1:c0 + 1 + P].squeeze(1),
                             M[0][64:P, 0:P]).then_inc(xst_set, 1)

                def stage_next():
                    nxt = Pos(at.g, at.u + 1) if at.u + 1 < UN else Pos(at.g + 1, 0)
                    wait(act, xst_set, f.back(1) if f else None, 2, 2)
                    wait(act, proj, at.back(1), 6, 6)
                    act.copy(xstage[:, nxt.u % 2, :],
                             xst[:, bass.ds(row(nxt), 1), nxt.u * P:nxt.u * P + P].squeeze(1)).then_inc(staged, 1)

                if f:
                    copy_weighed(0)
                    copy_weighed(1)
                if t:
                    for n in range(4):
                        copy_turned(n)
                if f:
                    shift_y1()
                if t:
                    carry_keys()
                if p:
                    for c in range(4):
                        copy_proj(c)
                    square(0)
                    square(1)
                if f:
                    scale_xn()
                if p:
                    copy_proj(4)
                    copy_proj(5)
                    stage_next()
                if f:
                    gelu()
                    copy_u()
                if t:
                    exps()
                if f:
                    shift_y2()

            run(act, step)

        @block.tensor
        def _(pe):
            pe.wait_ge(const_in, 32)
            pe.wait_ge(xw_in, 16 * 9)
            for a in range(4):
                last = pe.transpose(M[0][:, a * P:(a + 1) * P], wx[:, a, :] if a < 3 else cx, ident[:, :])
            last.then_inc(xw_turned, 1)
            pe.wait_ge(xw_copied, 1)
            ctxT = wxT[:, 3 * P:4 * P]
            pe.matmul(S[0][:, 0:P], ctxT, wxT[:, 2 * P:3 * P], start=True, stop=True)
            pe.matmul(M[1][:, 0:P], wxT[:, P:2 * P], ctxT, start=True, stop=True).then_inc(xkv, 1)
            for b in range(B):
                pe.wait_ge(xs_norm, UN * (b + 1))
                for u in range(UN):
                    last = pe.transpose((X + O)[b][:, u * P:(u + 1) * P], xn16[:, b * UN + u, :], ident[:, :])
                last.then_inc(xn_turned, 1)
            for b in range(B):
                pe.wait_ge(xn_copied, b + 1)
                pe.matmul((X + O)[b][:, :], wxT[:, 0:P], xnT16[:, b * N:(b + 1) * N], start=True, stop=True)\
                    .then_inc(xq, 1)
            pe.wait_ge(xk_set, 1)
            for b in range(B):
                pe.wait_ge(xq_set, b + 1)
                for u in range(UN):
                    c = (u * B + b) * NS
                    last = pe.matmul(S[1][:, c:c + NS], qTx[:, b * N + u * P:b * N + (u + 1) * P],
                                     kTx[:, b * NS:(b + 1) * NS], start=True, stop=True)
            last.then_inc(xsc, 1)
            pe.wait_ge(xp, 1)
            for u in range(UN):
                last = pe.transpose(M[0][:, u * P:(u + 1) * P], px[:, u * P:(u + 1) * P], ident[:, :])
            last.then_inc(xp_turned, 1)
            pe.wait_ge(xp_copied, 1)
            pe.wait_ge(xv_set, 1)
            for b in range(B):
                for u in range(UN):
                    last = pe.matmul((X + O)[b][:, u * P:(u + 1) * P],
                                     pxT[b * NS:(b + 1) * NS, u * P:(u + 1) * P],
                                     vx[b * NS:(b + 1) * NS, :], start=True, stop=True)
                last.then_inc(xatt, 1)
            for b in range(B):
                pe.wait_ge(x1_set, b + 1)
                pe.wait_ge(xs_norm, NT + UN * (b + 1))
                for u in range(UN):
                    last = pe.transpose((X + O)[b][:, u * P:(u + 1) * P], y[:, b * UN + u, :], ident[:, :])
                last.then_inc(y0_turned, 1)
            pe.wait_ge(y0_copied, 2 * B)
            pe.wait_ge(const_set, 4)

            def step(at, live):
                p, t, v, f = (at if live else None), lagged(at, 1), lagged(at, 2), lagged(at, 3)
                par = at.u % 2

                def project(c):
                    if c == 0:
                        wait(pe, staged, p, 1, 1)
                        pe.wait_ge(wqkv_in, layer(p) * 16 + 16)
                    if c < 2:
                        wait(pe, turned_copied, p.back(1), 5, c + 3)
                    else:
                        wait(pe, proj_copied, p, 6, c - 1)
                    w = wqkv[:, bass.ds(layer(p) % 2, 1), c * 512:(c + 1) * 512].squeeze(1)
                    pe.matmul(X[c % 2][:, :], xstage[:, par, :], w, start=True, stop=True).then_inc(proj, 1)

                def turn(n):
                    if n == 0:
                        wait(pe, qkr_set, t, 1, 1)
                    if n >= 2:
                        wait(pe, turned_copied, t, 5, n - 1)
                    else:
                        wait(pe, proj_copied, t, 6, n + 5)
                    for j in range(4):
                        c = (4 * n + j) * P
                        last = pe.transpose(X[n % 2][:, j * P:(j + 1) * P], qkr[:, c:c + P], ident[:, :])
                    last.then_inc(turned, 1)

                def score(e):
                    tp = t.u % 2
                    if e == 0:
                        wait(pe, turned_copied, t, 5, 4)
                        wait(pe, turned_copied, t.back(1), 5, 5)
                    wait(pe, less_max, t.back(1), 2, e + 1)
                    pe.matmul(S[e][:, :], identb[:, :], maskb[:, 0 if t.u == 0 else 1, :, :],
                              start=True, stop=False, skip_group_check=True)
                    for h in range(HP):
                        for w in range(QW):
                            last = pe.matmul(S[e][w * WIN:(w + 1) * WIN, h * 2 * WIN:(h + 1) * 2 * WIN],
                                             qT[64 * e:64 * e + 64, tp, h, w * WIN:(w + 1) * WIN],
                                             kT[64 * e:64 * e + 64, tp, h, w * WIN:(w + 2) * WIN],
                                             start=False, stop=True, skip_group_check=True)
                    last.then_inc(scored, 1)

                def weigh(w):
                    vp = v.u % 2
                    if w == -1 and v.u == 0:
                        return
                    first = w == (-1 if v.u else 0)
                    if first:
                        wait(pe, pT_set, v, 5, 5)
                        wait(pe, proj_copied, v, 6, 6)
                    q = w % QW
                    keys = slice(q * WIN, (q + 1) * WIN)
                    vu = (v.u - 1) % UN if w == -1 else v.u
                    j0, j1 = (WIN, 2 * WIN) if w == -1 else (0, WIN if w == QW - 1 else 2 * WIN)
                    t0 = max(w, 0) * WIN
                    for h in range(H):
                        e, hp = h % 2, h // 2
                        c = (hp % 4) * P + t0
                        if h % HP == 0 and first:
                            wait(pe, oT_set, v.back(1), 2, 1 + h // HP)
                        elif h % HP == 0:
                            if w == 0:
                                pe.wait_ge(edge_done, v.g * (2 * UN - 2) + (2 * v.u - 1 + h // HP))
                            else:
                                wait(pe, win_done, v, 2 * QW - 2, 2 * w - 1 + h // HP)
                        last = pe.matmul(O[hp // 4][64 * e:64 * e + 64, c:c + j1 - j0],
                                         vb[keys, vu, h * DH:(h + 1) * DH],
                                         pT[keys, vp, e * HP + hp, j0:j1],
                                         start=first and hp % 4 == 0, stop=True, skip_group_check=True)
                        if h % HP == HP - 1:
                            last.then_inc(edge_done if w == -1 else win_done if w < QW - 1 else weighed, 1)

                def out_proj():
                    wait(pe, oT_set, f, 2, 2)
                    wait(pe, xst_set, f.back(1), 2, 2)
                    pe.wait_ge(wrest_in, layer(f) * (16 * NREST) + 16 * NREST)
                    for h in range(HP):
                        last = pe.matmul(M[0][:, 0:D], oT[:, h, :],
                                         wo[:, bass.ds(layer(f) % 2, 1), h, :].squeeze(1),
                                         start=(h == 0), stop=(h == HP - 1))
                    last.then_inc(wo_done, 1)

                def turn_y1():
                    wait(pe, y1_set, f, 1, 1)
                    wait(pe, y2_set, f.back(1), 1, 1)
                    pe.transpose(M[1][:, 0:P], y1s[:, :], ident[:, :]).then_inc(y1_turned, 1)

                def turn_back():
                    wait(pe, fT_set, f, 2, 2)
                    pe.transpose(M[0][:, 0:P], fT[:, f.u * P:(f.u + 1) * P], ident[:, :]).then_inc(f_back, 1)

                def turn_xn():
                    wait(pe, xn_set, f, 1, 1)
                    pe.transpose(M[1][:, 0:P], xn[:, :], ident[:, :]).then_inc(xn_back, 1)

                def ffn_in():
                    wait(pe, xnT_set, f, 1, 1)
                    for n in (1, 0):
                        last = pe.matmul(M[n][:, 0:FI], xnT[:, :],
                                         w1[:, bass.ds(layer(f) % 2, 1), n * FI:(n + 1) * FI].squeeze(1),
                                         start=True, stop=True)
                    last.then_inc(h_done, 1)

                def turn_u():
                    wait(pe, hu_set, f, 1, 1)
                    for c, (f0, fn) in enumerate(FC):
                        last = pe.transpose(M[0][0:fn, c * P:(c + 1) * P], hu[:, f0:f0 + fn], ident[:, :])
                    last.then_inc(u_turned, 1)

                def ffn_out():
                    wait(pe, uT_set, f, 2, 2)
                    for c, (f0, fn) in enumerate(FC):
                        last = pe.matmul(M[1][:, 0:D], uT[0:fn, c, :],
                                         w2[0:fn, bass.ds(layer(f) % 2, 1), c, :].squeeze(1),
                                         start=(c == 0), stop=(c == len(FC) - 1))
                    last.then_inc(w2_done, 1)

                def turn_y2():
                    wait(pe, y2_set, f, 1, 1)
                    pe.transpose(M[0][:, 0:P], y2s[:, :], ident[:, :]).then_inc(y2_turned, 1)

                def project_all():
                    for c in range(6):
                        project(c)
                        if c == 3 and f:
                            turn_xn()

                if t:
                    turn(0)
                    turn(1)
                if f:
                    out_proj()
                if t:
                    turn(2)
                    turn(3)
                if f:
                    turn_y1()
                if v:
                    weigh(-1)
                if f:
                    turn_back()
                if p:
                    project_all()
                elif f:
                    turn_xn()
                if t:
                    score(0)
                if f:
                    ffn_in()
                if t:
                    score(1)
                if f:
                    turn_u()
                if v:
                    weigh(0)
                if f:
                    ffn_out()
                if v:
                    weigh(1)
                if f:
                    turn_y2()
                if v:
                    weigh(2)
                    weigh(3)

            run(pe, step)

        @block.vector
        def _(dve):
            dve.memset(mhalf[:, :], -0.5).then_inc(zero_set, 1)
            dve.memset(xst[:, :, 0:1], 0.0).then_inc(zero_set, 1)
            dve.memset(fT[:, 0:1], 0.0).then_inc(zero_set, 1)
            dve.memset(kT[:, 0, :, 0:WIN], 0.0).then_inc(zero_set, 1)

            def norm16(k, src, dst):
                for i in range(NT):
                    if k == 0 and i % UN == 0:
                        dve.wait_ge(x_in[i // UN], 16)
                    if k == 1 and i % UN == 0:
                        dve.wait_ge(x1_set, i // UN + 1)
                    dve.bn_stats(st16[:, i, :], src[:, i, :]).then_inc(xs_stat, 1)
                for i in range(NT):
                    dve.wait_ge(xs_stat, NT * k + i + 1)
                    dve.bn_aggr(mv16[:, i, :], st16[:, i, :]).then_inc(xs_aggr, 1)
                dve.wait_ge(xs_aggr, NT * (k + 1))
                dve.tensor_scalar(ve16[:, :], mv16[:, :, 1], 1e-5, None, ALU.add).then_inc(xs_ve, 1)
                dve.wait_ge(xs_rstd, k + 1)
                for i in range(NT):
                    dve.tensor_scalar(dst[:, i, :], src[:, i, :], mv16[:, i, 0:1], rs16[:, i:i + 1],
                                      ALU.subtract, ALU.mult).then_inc(xs_norm, 1)

            norm16(0, x1, xn16)
            dve.wait_ge(xw_in, 16 * 9)
            dve.wait_ge(xkv, 1)
            dve.tensor_tensor(vx, S[0][:, 0:P], bvb, ALU.add).then_inc(xv_set, 1)
            dve.wait_ge(const_in, 32)
            dve.tensor_copy(identb[:, :], ident[:, :]).then_inc(const_set, 1)
            for m in range(2):
                dve.tensor_copy(maskb[:, m, :, :], maskf[:, m, :].unsqueeze(1).to_broadcast([P, HP, 2 * WIN]))\
                    .then_inc(const_set, 1)
            sc = S[1][:, :].rearrange("p (a s) -> p a s", s=NS)
            e3 = ex0.rearrange("p (a s) -> p a s", s=NS)
            dve.wait_ge(xsc, 1)
            dve.tensor_reduce(smax[:, 0:NT], sc, AX.X, ALU.max).then_inc(xmax, 1)
            dve.wait_ge(xmax, 1)
            dve.tensor_tensor(e3, sc, smax[:, 0:NT].unsqueeze(2).to_broadcast([P, NT, NS]), ALU.subtract)\
                .then_inc(xsub, 1)
            dve.wait_ge(xexp, 1)
            dve.tensor_reduce(ssum[:, 0:NT], e3, AX.X, ALU.add).then_inc(xsum, 1)
            dve.wait_ge(xsum, 1)
            dve.reciprocal(rsum[:, 0:NT], ssum[:, 0:NT]).then_inc(xrec, 1)
            dve.wait_ge(xrec, 1)
            dve.tensor_tensor(px.rearrange("p (a s) -> p a s", s=NS), e3,
                              rsum[:, 0:NT].unsqueeze(2).to_broadcast([P, NT, NS]), ALU.mult).then_inc(xp, 1)
            dve.wait_ge(gate_set, 1)
            for b in range(B):
                dve.wait_ge(xatt, b + 1)
                xb = x1[:, b * UN:(b + 1) * UN, :].rearrange("p t d -> p (t d)")
                dve.scalar_tensor_tensor(xb, (X + O)[b][:, :], tgate[:, 0:1], xb, ALU.mult, ALU.add)\
                    .then_inc(x1_set, 1)
            norm16(1, x1, y)

            def step(at, live):
                p, t, f = (at if live else None), lagged(at, 1), lagged(at, 3)
                par = at.u % 2

                def turn_p():
                    vp = t.u % 2
                    wait(dve, p_set, t, 1, 1)
                    wait(dve, weighed, t.back(2), 2, 2)
                    dve.transpose(pT[:, vp, :, 0:WIN], pn[:, :, WIN:2 * WIN]).then_inc(pT_set, 1)
                    for w in range(QW):
                        q = (w - 1) % QW
                        dve.transpose(pT[q * WIN:(q + 1) * WIN, vp, :, WIN:2 * WIN],
                                      pn[w * WIN:(w + 1) * WIN, :, 0:WIN]).then_inc(pT_set, 1)

                def sum_squares():
                    for n in range(2):
                        wait(dve, squared, p, 2, n + 1)
                        if n == 0:
                            wait(dve, rn_set, p.back(2), 1, 1)
                        dve.tensor_reduce(ss[:, par, n * H:(n + 1) * H],
                                          sq[:, n * INNER:(n + 1) * INNER].rearrange("p (h d) -> p h d", d=DH),
                                          AX.X, ALU.add).then_inc(ss_set, 1)
                    wait(dve, ss_set, p, 3, 2)
                    dve.tensor_scalar(ss[:, par, :], ss[:, par, :], 1e-24, None, ALU.max).then_inc(ss_set, 1)

                q4 = qk[:, par, :].rearrange("p (a h d) -> p a h d", a=2, h=H)
                t14 = t1[:, :].rearrange("p (a h d) -> p a h d", a=2, h=H)
                t24 = t2[:, :].rearrange("p (a h d) -> p a h d", a=2, h=H)

                def table(kind, d0, dn):
                    tb = tab[:, bass.ds(layer(p), 1), at.u, kind:kind + 2, d0:d0 + dn].squeeze(1)
                    return tb.unsqueeze(2).to_broadcast([P, 2, H, dn])

                def rope_cos():
                    wait(dve, proj_copied, p, 6, 4)
                    wait(dve, qkr_set, p.back(1), 1, 1)
                    dve.tensor_tensor(t14, q4, table(0, 0, DH), ALU.mult).then_inc(roped, 1)

                def rope_sin(n):
                    o = (1 - n) * HALF
                    dve.tensor_tensor(t24[:, :, :, n * HALF:(n + 1) * HALF], q4[:, :, :, o:o + HALF],
                                      table(2, n * HALF, HALF), ALU.mult).then_inc(roped, 1)

                def rope_norm():
                    wait(dve, rope_sum, p, 2, 2)
                    wait(dve, rn_set, p, 1, 1)
                    wait(dve, turned, p.back(1), 4, 4)
                    dve.tensor_tensor(qkr[:, :].rearrange("p (a d) -> p a d", d=DH),
                                      t1[:, :].rearrange("p (a d) -> p a d", d=DH),
                                      rn[:, par, :].unsqueeze(2).to_broadcast([P, 2 * H, DH]), ALU.mult)\
                        .then_inc(qkr_set, 1)

                def row_max(e):
                    wait(dve, scored, t, 2, e + 1)
                    dve.tensor_reduce(smax[:, e * HP:(e + 1) * HP],
                                      S[e][:, :].rearrange("p (h j) -> p h j", h=HP), AX.X, ALU.max)\
                        .then_inc(max_set, 1)

                def subtract_max(e):
                    wait(dve, max_set, t, 2, e + 1)
                    if e == 0:
                        wait(dve, p_set, t.back(1), 1, 1)
                    dve.tensor_tensor(ex[:, e * HP:(e + 1) * HP, :],
                                      S[e][:, :].rearrange("p (h j) -> p h j", h=HP),
                                      smax[:, e * HP:(e + 1) * HP].unsqueeze(2)
                                      .to_broadcast([P, HP, 2 * WIN]), ALU.subtract).then_inc(less_max, 1)

                def sum_exp():
                    wait(dve, exp_set, t, 1, 1)
                    dve.tensor_reduce(ssum[:, :], ex[:, :, :], AX.X, ALU.add).then_inc(sum_set, 1)
                    wait(dve, sum_set, t, 1, 1)
                    wait(dve, p_set, t.back(1), 1, 1)
                    dve.reciprocal(rsum[:, :], ssum[:, :]).then_inc(rsum_set, 1)

                def add_y1():
                    wait(dve, wo_done, f, 1, 1)
                    wait(dve, y1b_set, f.back(1), 1, 1)
                    yt = y[:, bass.ds(row(f) * UN + f.u, 1), :].squeeze(1)
                    dve.tensor_tensor(y1s[:, :], M[0][:, 0:D], yt, ALU.add).then_inc(y1_set, 1)

                def stats():
                    wait(dve, f_back, f, 1, 1)
                    dve.bn_stats(st[:, :], M[0][:, 0:D]).then_inc(st_set, 1)
                    dve.wait_ge(zero_set, 4)
                    wait(dve, st_set, f, 1, 1)
                    dve.bn_aggr(mv[:, :], st[:, :]).then_inc(mv_set, 1)
                    wait(dve, mv_set, f, 1, 1)
                    wait(dve, rstd_set, f.back(1), 1, 1)
                    dve.tensor_scalar(ve[:, :], mv[:, 1:2], 1e-5, None, ALU.add).then_inc(ve_set, 1)

                def norm():
                    wait(dve, rstd_set, f, 1, 1)
                    dve.tensor_scalar(xn[:, :], M[0][:, 0:D], mv[:, 0:1], rstd[:, 0:1],
                                      ALU.subtract, ALU.mult).then_inc(xn_set, 1)

                def add_b1():
                    wait(dve, h_done, f, 1, 1)
                    for n, dst in ((1, hg), (0, ha)):
                        dve.tensor_tensor(dst[:, :], M[n][:, 0:FI],
                                          b1b[:, bass.ds(layer(f) % 2, 1), n * FI:(n + 1) * FI].squeeze(1),
                                          ALU.add).then_inc(hb_set, 1)

                def gate_u():
                    wait(dve, gelu_set, f, 1, 1)
                    wait(dve, hb_set, f, 2, 2)
                    dve.tensor_tensor(hu[:, :], ha[:, :], hg[:, :], ALU.mult).then_inc(hu_set, 1)

                def add_y2():
                    wait(dve, w2_done, f, 1, 1)
                    wait(dve, y1b_set, f, 1, 1)
                    wait(dve, y_kept, f.back(1), 1, 1)
                    dve.tensor_tensor(y2s[:, :], M[1][:, 0:D], y1b[:, :], ALU.add).then_inc(y2_set, 1)

                if f:
                    add_y1()
                    stats()
                    norm()
                if p:
                    if isinstance(at.g, int) and at.g == 0 and at.u == 0:
                        dve.wait_ge(tab_set, 6 * L)
                    rope_cos()
                    sum_squares()
                    rope_sin(0)
                    rope_sin(1)
                if t:
                    row_max(0)
                if f:
                    add_b1()
                if t:
                    subtract_max(0)
                if f:
                    gate_u()
                if t:
                    row_max(1)
                    subtract_max(1)
                    sum_exp()
                if f:
                    add_y2()
                if p:
                    rope_norm()
                if t:
                    turn_p()

            run(dve, step)
            for b in range(B):
                dve.wait_ge(y_kept, G * UN - (B - 1 - b) * UN)
                xb = x1[:, b * UN:(b + 1) * UN, :].rearrange("p t d -> p (t d)")
                dve.scalar_tensor_tensor(xb, y[:, b * UN:(b + 1) * UN, :].rearrange("p t d -> p (t d)"),
                                         tgate[:, 1:2], xb, ALU.mult, ALU.add).then_inc(x1_set, 1)

        @block.gpsimd
        def _(pool):
            pool.memset(kT[:, 1, :, 0:WIN], 0.0).then_inc(const_set, 1)
            pool.wait_ge(zero_set, 1)
            pool.wait_ge(xs_ve, 1)
            pool.tensor_tensor(rs16[:, :], ve16[:, :], mhalf[:, 0:NT], ALU.pow).then_inc(xs_rstd, 1)
            pool.wait_ge(rope_in, 16 * 5)

            def scale_tables(l):
                for a in range(2):
                    pool.tensor_tensor(tab[:, l, :, a, :], ropeb[:, :, a, :],
                                       qks[:, a, l, :].unsqueeze(1).to_broadcast([P, UN, DH]), ALU.mult)\
                        .then_inc(tab_set, 1)
                    for n in range(2):
                        o = (1 - n) * HALF
                        pool.tensor_tensor(tab[:, l, :, 2 + a, n * HALF:(n + 1) * HALF],
                                           ropeb[:, :, 2 + a, n * HALF:(n + 1) * HALF],
                                           qks[:, a, l, o:o + HALF].unsqueeze(1).to_broadcast([P, UN, HALF]),
                                           ALU.mult).then_inc(tab_set, 1)

            for l in range(L):
                if l == 3:
                    pool.wait_ge(xs_ve, 2)
                    pool.tensor_tensor(rs16[:, :], ve16[:, :], mhalf[:, 0:NT], ALU.pow).then_inc(xs_rstd, 1)
                scale_tables(l)

            def step(at, live):
                p, t, f = (at if live else None), lagged(at, 1), lagged(at, 3)
                par = at.u % 2
                if f:
                    pool.wait_ge(wrest_in, 16 * NREST)
                    wait(pool, y1_set, f, 1, 1)
                    wait(pool, y2_set, f.back(1), 1, 1)
                    pool.tensor_tensor(y1b[:, :], y1s[:, :],
                                       b2b[:, bass.ds(layer(f) % 2, 1), :].squeeze(1), ALU.add).then_inc(y1b_set, 1)
                    wait(pool, ve_set, f, 1, 1)
                    wait(pool, xn_set, f.back(1), 1, 1)
                    pool.tensor_tensor(rstd[:, :], ve[:, :], mhalf[:, 0:1], ALU.pow).then_inc(rstd_set, 1)
                if p:
                    wait(pool, ss_set, p, 3, 3)
                    wait(pool, qkr_set, p.back(2), 1, 1)
                    pool.tensor_tensor(rn[:, par, :], ss[:, par, :], mhalf[:, :], ALU.pow).then_inc(rn_set, 1)
                    wait(pool, roped, p, 3, 3)
                    for n in range(2):
                        pool.tensor_tensor(t1[:, n * INNER:(n + 1) * INNER], t1[:, n * INNER:(n + 1) * INNER],
                                           t2[:, n * INNER:(n + 1) * INNER], ALU.add).then_inc(rope_sum, 1)
                if t:
                    wait(pool, rsum_set, t, 1, 1)
                    wait(pool, pT_set, t.back(1), 5, 5)
                    pool.tensor_tensor(pn[:, :, :], ex[:, :, :],
                                       rsum[:, :].unsqueeze(2).to_broadcast([P, H, 2 * WIN]), ALU.mult)\
                        .then_inc(p_set, 1)
                if f:
                    wait(pool, y2_set, f, 1, 1)
                    pool.tensor_copy(y[:, bass.ds(row(f) * UN + f.u, 1), :].squeeze(1), y2s[:, :])\
                        .then_inc(y_kept, 1)

            run(pool, step)


_INS = ["x", "ctx_1024", "g_xattn", "g_ffn", "L0_xattn_Wq", "L0_xattn_bq", "L0_xattn_Wk", "L0_xattn_bk",
        "L0_xattn_Wv", "L0_xattn_bv", "L0_ffn_Wqkv", "L0_ffn_q_scale", "L0_ffn_k_scale", "L0_ffn_Wo",
        "L0_ffn_ln_g", "L0_ffn_ln_b", "L0_ffn_W1", "L0_ffn_b1", "L0_ffn_W2", "L0_ffn_b2"]


def _constants(n, dh):
    import numpy as np

    f = np.float32
    half = np.arange(0, dh, 2, dtype=f)
    inv_freq = (f(1.0) / f(10000.0) ** (half / f(dh))).astype(f)
    t = np.arange(n, dtype=f)
    freqs = (t[:, None] * inv_freq[None, :]).astype(f)
    base = ((half + f(0.4 * dh)) / f(1.4 * dh)).astype(f)
    scale = (base[None, :] ** ((t - n // 2) / f(WIN // 2))[:, None]).astype(f)
    cos, sin = np.cos(freqs), np.sin(freqs)
    inv = f(1.0) / scale
    kinds = [np.concatenate([a * m, b * m], -1) for a, b, m in
             ((cos, cos, scale * f(8.0)), (cos, cos, inv), (-sin, sin, scale * f(8.0)), (-sin, sin, inv))]
    rope = np.stack(kinds, 1).reshape(n // P, P, 4, dh).transpose(1, 0, 2, 3)
    i = (np.arange(P) % WIN)[:, None]
    j = np.arange(WIN)[None, :]
    low = f(-3.0e38)
    own = np.where(j > i, low, f(0))
    before = np.where(j < i, low, f(0))
    first = np.where((np.arange(P) < WIN)[:, None], low, before)
    masks = np.stack([np.concatenate([first, own], 1), np.concatenate([before, own], 1)], 1)
    return [np.ascontiguousarray(a, dtype=f) for a in (rope, masks, np.eye(P))]


def kernel(**inputs):
    import numpy as _np
    import concourse.bacc as _bacc
    from concourse import mybir as _mybir
    from concourse.bass_utils import run_bass_kernel_spmd as _run

    nc = _bacc.Bacc("TRN2", target_bir_lowering=False, num_devices=1)
    arrays, args = {}, []
    named = [(n, inputs[n]) for n in _INS]
    named += list(zip(("rope", "masks", "ident"), _constants(inputs["x"].shape[1], inputs["L0_ffn_q_scale"].shape[1])))
    for name, a in named:
        if name in ("L0_ffn_ln_g", "L0_ffn_ln_b"):
            a = _np.asarray(a).T
        a = _np.ascontiguousarray(a)
        arrays[f"in_{name}_dram"] = a
        args.append(nc.dram_tensor(f"in_{name}_dram", a.shape, _mybir.dt.from_np(a.dtype), kind="ExternalInput").ap())
    args.append(nc.dram_tensor("out_dram", inputs["x"].shape, _mybir.dt.float32, kind="ExternalOutput").ap())
    build(nc, *args)
    return _run(nc, [arrays], core_ids=[0]).results[0]["out_dram"]
```

```python
from contextlib import ExitStack

import concourse.bass as bass
from concourse import mybir

ALU = mybir.AluOpType
ACT = mybir.ActivationFunctionType
AX = mybir.AxisListType
F32 = mybir.dt.float32
BF16 = mybir.dt.bfloat16

P = 128
WIN = 32
QW = P // WIN
UN = 4


class Pos:

    def __init__(self, g, u):
        self.g, self.u = g, u

    def back(self, lag):
        d = (lag - self.u + UN - 1) // UN if lag > self.u else 0
        if isinstance(self.g, int) and self.g - d < 0:
            return None
        return Pos(self.g - d if d else self.g, self.u - lag + UN * d)

    def count(self, per, k):
        return self.g * (UN * per) + (self.u * per + k) if not isinstance(self.g, int) \
            else (self.g * UN + self.u) * per + k


def build(nc, x, ctx_in, g_xattn, g_ffn, Wq, bq, Wk, bk, Wv, bv, Wqkv, q_scale, k_scale, Wo, ln_g, ln_b,
          W1, b1, W2, b2, rope, masks, ident_in, out):
    B, N, D = x.shape
    NS = ctx_in.shape[1]
    L = Wqkv.shape[0]
    INNER = Wo.shape[1]
    DH = q_scale.shape[1]
    H = INNER // DH
    HP = H // 2
    HALF = DH // 2
    FI = W2.shape[1]
    FC = [(c, min(P, FI - c)) for c in range(0, FI, P)]
    NT = B * N // P
    G = L * B
    assert N == UN * P and D == P and B * NS == P and H * DH == 2 * 512 and NS == WIN
    NREST = 4 + len(FC)
    GL = 2

    with ExitStack() as ctx:
        def sb(name, shape, dt=F32):
            return ctx.enter_context(nc.sbuf_tensor(name, shape, dt))

        def bank(name):
            return ctx.enter_context(nc.psum_tensor(name, [P, 512], F32))

        def sem(name):
            return ctx.enter_context(nc.semaphore(name))

        X = [bank("px0"), bank("px1")]
        S = [bank("ps0"), bank("ps1")]
        O = [bank("po0"), bank("po1")]
        M = [bank("pm0"), bank("pm1")]

        wqkv = sb("wqkv", [P, 2, 3 * INNER])
        wo = sb("wo", [P, 2, HP, D])
        w1 = sb("w1", [P, 2, 2 * FI])
        w2 = sb("w2", [P, 2, len(FC), D])
        b1b = sb("b1b", [P, 2, 2 * FI])
        b2b = sb("b2b", [P, 2, D])
        lng = sb("lng", [P, L])
        lnb = sb("lnb", [P, L])
        tab = sb("tab", [P, L, UN, 4, DH])
        maskb = sb("maskb", [P, 2, HP, 2 * WIN], BF16)
        ident = sb("ident", [P, P])
        identb = sb("identb", [P, P], BF16)
        mhalf = sb("mhalf", [P, 2 * H])
        y = sb("y", [P, NT, D])
        x1 = sb("x1", [P, NT, D])
        xst = sb("xst", [P, B, N + 1])
        xstage = sb("xstage", [P, UN, P])
        qk = sb("qk", [P, 2, 2 * INNER])
        vb = sb("vb", [P, UN, INNER])
        sq = sb("sq", [P, 2 * INNER])
        t1 = sb("t1", [P, 2 * INNER])
        t2 = sb("t2", [P, 2 * INNER])
        qkr = sb("qkr", [P, 2 * INNER])
        ss = sb("ss", [P, 2, 2 * H])
        rn = sb("rn", [P, 2, 2 * H])
        qT = sb("qT", [P, 2, HP, P])
        kT = sb("kT", [P, 2, HP, WIN + P])
        smax = sb("smax", [P, H])
        ex = sb("ex", [P, H, 2 * WIN])
        ssum = sb("ssum", [P, H])
        rsum = sb("rsum", [P, H])
        pn = ex
        pT = sb("pT", [P, H, P])
        oT = sb("oT", [P, HP, P])
        y1s = sb("y1s", [P, D])
        y1b = sb("y1b", [P, 2, D])
        y2s = sb("y2s", [P, D])
        fT = sb("fT", [P, N + 1])
        st = sb("st", [P, 6])
        mv = sb("mv", [P, 2])
        ve = sb("ve", [P, 1])
        rstd = sb("rstd", [P, 1])
        xn = sb("xn", [P, D])
        xnT = sb("xnT", [P, P])
        ha = sb("ha", [P, FI])
        hg = sb("hg", [P, FI])
        hu = ha
        uT = sb("uT", [P, len(FC), P])
        gates = sb("gates", [P, 2])
        tgate = sb("tgate", [P, 2])
        bqk = sb("bqk", [P, 2])
        ropeb = pn[:, :, :].rearrange("p h j -> p (h j)").rearrange("p (u k d) -> p u k d", u=UN, k=4)
        qks = oT[:, 0:2 * L * DH // P, :].rearrange("p h t -> p (h t)").rearrange("p (a l d) -> p a l d", a=2, l=L)
        maskf = oT[:, HP - 1, :].rearrange("p (m j) -> p m j", m=2)
        early = sq[:, 0:10 * NT]
        st16 = early[:, 0:6 * NT].rearrange("p (t k) -> p t k", k=6)
        mv16 = early[:, 6 * NT:8 * NT].rearrange("p (t k) -> p t k", k=2)
        ve16 = early[:, 8 * NT:9 * NT]
        rs16 = early[:, 9 * NT:10 * NT]
        xn16 = t1[:, :].rearrange("p (t d) -> p t d", d=D)
        xnT16 = t2[:, :]
        qTx = qkr[:, :]
        wx = qk[:, 0, 0:3 * P].rearrange("p (a d) -> p a d", a=3)
        cx = qk[:, 0, 3 * P:4 * P]
        wxT = qk[:, 0, 4 * P:8 * P]
        kTx = qk[:, 0, 8 * P:9 * P]
        vx = qk[:, 0, 9 * P:10 * P]
        bvb = qk[:, 0, 10 * P:11 * P]
        ex0 = qk[:, 1, 0:512]
        px = qk[:, 1, 512:1024]
        pxT = qk[:, 1, 1024:1536]

        x_in = [sem(f"x_in{b}") for b in range(B)]
        xw_in, const_in, rope_in = sem("xw_in"), sem("const_in"), sem("rope_in")
        wqkv_in, wrest_in = sem("wqkv_in"), sem("wrest_in")
        stored = sem("stored")
        const_set, zero_set, tab_set = sem("const_set"), sem("zero_set"), sem("tab_set")
        xs_stat, xs_aggr, xs_ve, xs_rstd, xs_norm = (sem(n) for n in
                                                     ("xs_stat", "xs_aggr", "xs_ve", "xs_rstd", "xs_norm"))
        xw_turned, xw_copied, xkv, xk_set, xv_set = (sem(n) for n in
                                                     ("xw_turned", "xw_copied", "xkv", "xk_set", "xv_set"))
        xn_turned, xn_copied, xq, xq_set, xsc = (sem(n) for n in ("xn_turned", "xn_copied", "xq", "xq_set", "xsc"))
        xmax, xsub, xexp, xsum, xrec, xp = (sem(n) for n in ("xmax", "xsub", "xexp", "xsum", "xrec", "xp"))
        xp_turned, xp_copied, xatt, gate_set, x1_set = (sem(n) for n in
                                                        ("xp_turned", "xp_copied", "xatt", "gate_set", "x1_set"))
        y0_turned, y0_copied = sem("y0_turned"), sem("y0_copied")
        staged = sem("staged")
        qk_done = sem("qk_done")
        qk_copied = sem("qk_copied")
        v_done = sem("v_done")
        v_copied = sem("v_copied")
        squared = sem("squared")
        ss_set = sem("ss_set")
        rn_set = sem("rn_set")
        roped = sem("roped")
        rope_sum = sem("rope_sum")
        qkr_set = sem("qkr_set")
        turned = sem("turned")
        turned_copied = sem("turned_copied")
        scored = sem("scored")
        max_set = sem("max_set")
        less_max = sem("less_max")
        exp_set = sem("exp_set")
        sum_set = sem("sum_set")
        rsum_set = sem("rsum_set")
        p_set = sem("p_set")
        pT_zero = sem("pT_zero")
        pT_set = sem("pT_set")
        tail_done = sem("tail_done")
        weighed = sem("weighed")
        oT_set = sem("oT_set")
        wo_done = sem("wo_done")
        y1_set = sem("y1_set")
        y1b_set = sem("y1b_set")
        y1_turned = sem("y1_turned")
        fT_set = sem("fT_set")
        f_back = sem("f_back")
        st_set, mv_set, ve_set = sem("st_set"), sem("mv_set"), sem("ve_set")
        rstd_set = sem("rstd_set")
        xn_set = sem("xn_set")
        xn_back = sem("xn_back")
        xnT_set = sem("xnT_set")
        h_done = sem("h_done")
        hb_set = sem("hb_set")
        gelu_set = sem("gelu_set")
        hu_set = sem("hu_set")
        u_turned = sem("u_turned")
        uT_set = sem("uT_set")
        w2_done = sem("w2_done")
        y2_set = sem("y2_set")
        y_kept = sem("y_kept")
        y2_turned = sem("y2_turned")
        xst_set = sem("xst_set")

        def wait(eng, s, at, per, k):
            if at is not None:
                eng.wait_ge(s, at.count(per, k))

        def layer(at):
            return at.g // B

        def row(at):
            return at.g % B

        LAST = 6

        def run(eng, step):
            for g in range(GL):
                for u in range(UN):
                    step(Pos(g, u), True)
            with eng.Fori(GL, G) as g:
                for u in range(UN):
                    step(Pos(g, u), True)
            for k in range(LAST):
                step(Pos(G + k // UN, k % UN), False)

        def lagged(at, lag):
            p = at.back(lag)
            return p if p is None or not isinstance(p.g, int) or p.g < G else None

        block = ctx.enter_context(nc.Block())

        @block.sync
        def _(sp):
            sp.dma_start(ident[:, :], ident_in).then_inc(const_in, 16)
            for b in range(B):
                sp.dma_start(x1[:, b * UN:(b + 1) * UN, :],
                             x[b].rearrange("(t p) d -> p t d", p=P)).then_inc(x_in[b], 16)
            for a, w in enumerate((Wq, Wk, Wv)):
                sp.dma_start(wx[:, a, :], w).then_inc(xw_in, 16)
            sp.dma_start(cx, ctx_in.rearrange("b s d -> (b s) d")).then_inc(xw_in, 16)
            sp.dma_start(bvb, bv.partition_broadcast(P)).then_inc(xw_in, 16)
            sp.dma_start(bqk[:, 0:1], bq.unsqueeze(1)).then_inc(xw_in, 16)
            sp.dma_start(bqk[:, 1:2], bk.unsqueeze(1)).then_inc(xw_in, 16)
            sp.dma_start(gates[:, 0:1], g_xattn.partition_broadcast(P)).then_inc(xw_in, 16)
            sp.dma_start(gates[:, 1:2], g_ffn.partition_broadcast(P)).then_inc(xw_in, 16)
            sp.dma_start(maskf[:, :, :], masks).then_inc(const_in, 16)
            sp.dma_start(ropeb[:, :, :, :], rope).then_inc(rope_in, 16)
            sp.dma_start(qks[:, 0, :, :], q_scale.partition_broadcast(P)).then_inc(rope_in, 16)
            sp.dma_start(qks[:, 1, :, :], k_scale.partition_broadcast(P)).then_inc(rope_in, 16)
            sp.dma_start(lng[:, :], ln_g).then_inc(rope_in, 16)
            sp.dma_start(lnb[:, :], ln_b).then_inc(rope_in, 16)

            for l in range(L):
                h = l % 2
                if l >= 1:
                    sp.wait_ge(wqkv_in, 16 * l)
                    sp.wait_ge(wrest_in, 16 * NREST * l)
                if l >= 2:
                    sp.wait_ge(y2_set, NT * (l - 1))
                sp.dma_start(wqkv[:, h, :], Wqkv[l]).then_inc(wqkv_in, 16)
                sp.dma_start(wo[:, h, :, :], Wo[l].rearrange("(h p) d -> p h d", p=P)).then_inc(wrest_in, 16)
                sp.dma_start(w1[:, h, :], W1[l]).then_inc(wrest_in, 16)
                for c, (f0, fn) in enumerate(FC):
                    sp.dma_start(w2[0:fn, h, c, :], W2[l, f0:f0 + fn, :]).then_inc(wrest_in, 16)
                sp.dma_start(b1b[:, h, :], b1[l].partition_broadcast(P)).then_inc(wrest_in, 16)
                sp.dma_start(b2b[:, h, :], b2[l].partition_broadcast(P)).then_inc(wrest_in, 16)
            for b in range(B):
                sp.wait_ge(x1_set, B + b + 1)
                sp.dma_start(out[b].rearrange("(t p) d -> p t d", p=P),
                             x1[:, b * UN:(b + 1) * UN, :]).then_inc(stored, 16)
            sp.wait_ge(stored, 16 * B)

        @block.scalar
        def _(act):
            act.wait_ge(xw_in, 16 * 9)
            act.activation(tgate[:, :], gates[:, :], ACT.Tanh).then_inc(gate_set, 1)
            act.wait_ge(xw_turned, 1)
            act.copy(wxT, M[0][:, :]).then_inc(xw_copied, 1)
            act.wait_ge(xkv, 1)
            act.activation(kTx, M[1][:, 0:P], ACT.Identity, bias=bqk[:, 1:2]).then_inc(xk_set, 1)
            for b in range(B):
                act.wait_ge(xn_turned, b + 1)
                act.copy(xnT16[:, b * N:(b + 1) * N], (X + O)[b][:, :]).then_inc(xn_copied, 1)
            for b in range(B):
                act.wait_ge(xq, b + 1)
                act.activation(qTx[:, b * N:(b + 1) * N], (X + O)[b][:, :], ACT.Identity,
                               bias=bqk[:, 0:1]).then_inc(xq_set, 1)
            act.wait_ge(xsub, 1)
            act.activation(ex0, ex0, ACT.Exp).then_inc(xexp, 1)
            act.wait_ge(xp_turned, 1)
            act.copy(pxT, M[0][:, :]).then_inc(xp_copied, 1)
            act.wait_ge(zero_set, 4)
            for b in range(B):
                act.wait_ge(y0_turned, b + 1)
                act.copy(xst[0:64, b, 0:N], (X + O)[b][0:64, :]).then_inc(y0_copied, 1)
                act.copy(xst[64:P, b, 1:N + 1], (X + O)[b][64:P, :]).then_inc(y0_copied, 1)
            act.wait_ge(y0_copied, 2)
            act.copy(xstage[:, 0, :], xst[:, 0, 0:P]).then_inc(staged, 1)

            def step(at, live):
                p, r, n, t, f, e = (at if live else None), *(lagged(at, k) for k in (1, 2, 3, 5, 6))

                def copy_weighed(k):
                    wait(act, weighed, f, 4, 2 * k + 2)
                    wait(act, wo_done, f.back(1), 1, 1)
                    act.copy(oT[:, 4 * k:4 * k + 4, :],
                             O[k][:, :].rearrange("p (h t) -> p h t", h=4)).then_inc(oT_set, 1)

                def square(k):
                    wait(act, qk_copied, r, 4, 2 * k + 2)
                    wait(act, ss_set, r.back(1), 3, 2)
                    act.activation(sq[:, k * INNER:(k + 1) * INNER], qk[:, r.u % 2, k * INNER:(k + 1) * INNER],
                                   ACT.Square).then_inc(squared, 1)

                def scale_xn():
                    l = layer(e)
                    act.wait_ge(rope_in, 16 * 5)
                    wait(act, xn_back, e, 1, 1)
                    act.activation(xnT[:, :], M[1][:, 0:P], ACT.Identity, scale=lng[:, bass.ds(l, 1)],
                                   bias=lnb[:, bass.ds(l, 1)]).then_inc(xnT_set, 1)

                def exps():
                    wait(act, less_max, t, 2, 2)
                    act.activation(ex[:, :, :], ex[:, :, :], ACT.Exp).then_inc(exp_set, 1)

                def copy_qk(c):
                    wait(act, qk_done, p, 4, c + 1)
                    if c == 0:
                        wait(act, roped, p.back(2), 3, 3)
                    act.copy(qk[:, p.u % 2, c * 512:(c + 1) * 512], X[c % 2][:, :]).then_inc(qk_copied, 1)

                def shift_y1():
                    c0 = P * f.u
                    wait(act, y1_turned, f, 1, 1)
                    act.copy(fT[0:64, c0:c0 + P], M[0][0:64, 0:P]).then_inc(fT_set, 1)
                    act.copy(fT[64:P, c0 + 1:c0 + 1 + P], M[0][64:P, 0:P]).then_inc(fT_set, 1)

                def gelu():
                    wait(act, hb_set, e, 2, 1)
                    act.activation(hg[:, :], hg[:, :], ACT.Gelu).then_inc(gelu_set, 1)

                def copy_turned(k):
                    wait(act, turned, n, 4, k + 1)
                    if k == 0:
                        wait(act, scored, n.back(2), 2, 2)
                    src = X[k % 2][:, :].rearrange("p (h t) -> p h t", h=4)
                    dst = (qT[:, n.u % 2, 4 * k:4 * k + 4, :] if k < 2
                           else kT[:, n.u % 2, 4 * k - 8:4 * k - 4, WIN:WIN + P])
                    act.copy(dst, src).then_inc(turned_copied, 1)

                def carry_keys():
                    wait(act, turned_copied, n, 5, 4)
                    wait(act, scored, n.back(1), 2, 2)
                    act.copy(kT[:, 1 - n.u % 2, :, 0:WIN], kT[:, n.u % 2, :, P:P + WIN]).then_inc(turned_copied, 1)

                def copy_v(c):
                    wait(act, v_done, n, 2, c + 1)
                    if c == 0:
                        wait(act, weighed, n.back(3), 4, 4)
                    act.copy(vb[:, n.u, c * 512:(c + 1) * 512], X[c][:, :]).then_inc(v_copied, 1)

                def copy_u():
                    wait(act, u_turned, e, 1, 1)
                    nf = len(FC) - 1
                    act.copy(uT[:, 0:nf, :], M[1][:, 0:nf * P].rearrange("p (c t) -> p c t", c=nf)).then_inc(uT_set, 1)
                    act.copy(uT[0:FC[nf][1], nf, :], M[1][0:FC[nf][1], nf * P:(nf + 1) * P]).then_inc(uT_set, 1)

                def shift_y2():
                    c0 = P * e.u
                    wait(act, y2_turned, e, 1, 1)
                    b = row(e)
                    act.copy(xst[0:64, bass.ds(b, 1), c0:c0 + P].squeeze(1), M[1][0:64, 0:P]).then_inc(xst_set, 1)
                    act.copy(xst[64:P, bass.ds(b, 1), c0 + 1:c0 + 1 + P].squeeze(1),
                             M[1][64:P, 0:P]).then_inc(xst_set, 1)
                    act.copy(y[:, bass.ds(b * UN + e.u, 1), :].squeeze(1), y2s[:, :]).then_inc(y_kept, 1)

                def stage_next():
                    nxt = Pos(at.g, at.u + 1) if at.u + 1 < UN else Pos(at.g + 1, 0)
                    wait(act, xst_set, e.back(1) if e else None, 2, 2)
                    wait(act, v_done, at.back(3), 2, 2)
                    act.copy(xstage[:, nxt.u, :],
                             xst[:, bass.ds(row(nxt), 1), nxt.u * P:nxt.u * P + P].squeeze(1)).then_inc(staged, 1)

                if f:
                    copy_weighed(0)
                if f:
                    copy_weighed(1)
                if p:
                    copy_qk(0)
                if r:
                    square(0)
                if r:
                    square(1)
                if e:
                    scale_xn()
                if p:
                    copy_qk(1)
                if t:
                    exps()
                if e:
                    gelu()
                if p:
                    copy_qk(2)
                if f:
                    shift_y1()
                if p:
                    copy_qk(3)
                if n:
                    copy_turned(0)
                if n:
                    copy_turned(1)
                if n:
                    copy_turned(2)
                if n:
                    copy_turned(3)
                if n:
                    carry_keys()
                if e:
                    copy_u()
                if n:
                    copy_v(0)
                if n:
                    copy_v(1)
                if e:
                    shift_y2()
                if p:
                    stage_next()

            run(act, step)

        @block.tensor
        def _(pe):
            pe.wait_ge(const_in, 32)
            pe.wait_ge(xw_in, 16 * 9)
            for a in range(4):
                last = pe.transpose(M[0][:, a * P:(a + 1) * P], wx[:, a, :] if a < 3 else cx, ident[:, :])
            last.then_inc(xw_turned, 1)
            pe.wait_ge(xw_copied, 1)
            ctxT = wxT[:, 3 * P:4 * P]
            pe.matmul(S[0][:, 0:P], ctxT, wxT[:, 2 * P:3 * P], start=True, stop=True)
            pe.matmul(M[1][:, 0:P], wxT[:, P:2 * P], ctxT, start=True, stop=True).then_inc(xkv, 1)
            for b in range(B):
                pe.wait_ge(xs_norm, UN * (b + 1))
                for u in range(UN):
                    last = pe.transpose((X + O)[b][:, u * P:(u + 1) * P], xn16[:, b * UN + u, :], ident[:, :])
                last.then_inc(xn_turned, 1)
            for b in range(B):
                pe.wait_ge(xn_copied, b + 1)
                pe.matmul((X + O)[b][:, :], wxT[:, 0:P], xnT16[:, b * N:(b + 1) * N], start=True, stop=True)\
                    .then_inc(xq, 1)
            pe.wait_ge(xk_set, 1)
            for b in range(B):
                pe.wait_ge(xq_set, b + 1)
                for u in range(UN):
                    c = (u * B + b) * NS
                    last = pe.matmul(S[1][:, c:c + NS], qTx[:, b * N + u * P:b * N + (u + 1) * P],
                                     kTx[:, b * NS:(b + 1) * NS], start=True, stop=True)
            last.then_inc(xsc, 1)
            pe.wait_ge(xp, 1)
            for u in range(UN):
                last = pe.transpose(M[0][:, u * P:(u + 1) * P], px[:, u * P:(u + 1) * P], ident[:, :])
            last.then_inc(xp_turned, 1)
            pe.wait_ge(xp_copied, 1)
            pe.wait_ge(xv_set, 1)
            for b in range(B):
                for u in range(UN):
                    last = pe.matmul((X + O)[b][:, u * P:(u + 1) * P],
                                     pxT[b * NS:(b + 1) * NS, u * P:(u + 1) * P],
                                     vx[b * NS:(b + 1) * NS, :], start=True, stop=True)
                last.then_inc(xatt, 1)
            for b in range(B):
                pe.wait_ge(x1_set, b + 1)
                pe.wait_ge(xs_norm, NT + UN * (b + 1))
                for u in range(UN):
                    last = pe.transpose((X + O)[b][:, u * P:(u + 1) * P], y[:, b * UN + u, :], ident[:, :])
                last.then_inc(y0_turned, 1)
            pe.wait_ge(y0_copied, 2 * B)
            pe.wait_ge(const_set, 4)

            def step(at, live):
                p, n, t, v, f, e = (at if live else None), *(lagged(at, k) for k in (2, 3, 4, 5, 6))
                prev = at.back(1)

                def project_qk(c):
                    if c == 0:
                        wait(pe, staged, p, 1, 1)
                        pe.wait_ge(wqkv_in, layer(p) * 16 + 16)
                    if c < 2:
                        wait(pe, qk_copied, prev, 4, c + 3)
                        wait(pe, v_copied, at.back(3), 2, c + 1)
                    else:
                        wait(pe, qk_copied, p, 4, c - 1)
                    w = wqkv[:, bass.ds(layer(p) % 2, 1), c * 512:(c + 1) * 512].squeeze(1)
                    pe.matmul(X[c % 2][:, :], xstage[:, p.u, :], w, start=True, stop=True).then_inc(qk_done, 1)

                def turn(k):
                    if k == 0:
                        wait(pe, qkr_set, n, 2, 2)
                    if k >= 2:
                        wait(pe, turned_copied, n, 5, k - 1)
                    elif p:
                        wait(pe, qk_copied, p, 4, k + 3)
                    else:
                        wait(pe, v_copied, n.back(1), 2, k + 1)
                    for j in range(4):
                        c = (4 * k + j) * P
                        last = pe.transpose(X[k % 2][:, j * P:(j + 1) * P], qkr[:, c:c + P], ident[:, :])
                    last.then_inc(turned, 1)

                def project_v(c):
                    wait(pe, turned_copied, n, 5, c + 3)
                    w = wqkv[:, bass.ds(layer(n) % 2, 1), 2 * INNER + c * 512:2 * INNER + (c + 1) * 512].squeeze(1)
                    pe.matmul(X[c][:, :], xstage[:, n.u, :], w, start=True, stop=True).then_inc(v_done, 1)

                def score(q):
                    tp = t.u % 2
                    if q == 0:
                        wait(pe, turned_copied, t, 5, 4)
                        wait(pe, turned_copied, t.back(1), 5, 5)
                    wait(pe, less_max, t.back(1), 2, q + 1)
                    pe.matmul(S[q][:, :], identb[:, :], maskb[:, 0 if t.u == 0 else 1, :, :],
                              start=True, stop=False, skip_group_check=True)
                    for h in range(HP):
                        for w in range(QW):
                            last = pe.matmul(S[q][w * WIN:(w + 1) * WIN, h * 2 * WIN:(h + 1) * 2 * WIN],
                                             qT[64 * q:64 * q + 64, tp, h, w * WIN:(w + 1) * WIN],
                                             kT[64 * q:64 * q + 64, tp, h, w * WIN:(w + 2) * WIN],
                                             start=False, stop=True, skip_group_check=True)
                    last.then_inc(scored, 1)

                def weigh_tail(i, hq, u, w, first):
                    par, hp = i % 2, 4 * (i // 2) + hq
                    keys = slice(P - WIN, P)
                    c = hq * P + w * WIN
                    return pe.matmul(O[i // 2][64 * par:64 * par + 64, c:c + WIN],
                                     vb[keys, u, (2 * hp + par) * DH:(2 * hp + par + 1) * DH],
                                     pT[keys, par * HP + hp, w * WIN:(w + 1) * WIN],
                                     start=first, stop=True, skip_group_check=True)

                def weigh_tails():
                    wait(pe, pT_set, v, 8, 8)
                    wait(pe, v_copied, v, 2, 2)
                    wait(pe, oT_set, v.back(1), 2, 2)
                    for hq in range(4):
                        for i in range(4):
                            last = weigh_tail(i, hq, v.u, QW - 1, hq == 0)
                            if hq == 3 and v.u == 0:
                                last.then_inc(tail_done, 1)
                    if v.u:
                        for hq in range(4):
                            for i in range(4):
                                last = weigh_tail(i, hq, v.u - 1, 0, False)
                                if hq == 3:
                                    last.then_inc(tail_done, 1)

                def weigh():
                    keys = slice(0, P - WIN)
                    for hq in range(4):
                        for i in range(4):
                            if hq == 0:
                                wait(pe, tail_done, v, 4, i + 1)
                            par, hp = i % 2, 4 * (i // 2) + hq
                            last = pe.matmul(O[i // 2][64 * par:64 * par + 64, hq * P:(hq + 1) * P],
                                             vb[keys, v.u, (2 * hp + par) * DH:(2 * hp + par + 1) * DH],
                                             pT[keys, par * HP + hp, :],
                                             start=False, stop=True, skip_group_check=True)
                            if hq == 3:
                                last.then_inc(weighed, 1)

                def out_proj():
                    wait(pe, oT_set, f, 2, 2)
                    wait(pe, xn_set, f.back(1), 1, 1)
                    pe.wait_ge(wrest_in, layer(f) * (16 * NREST) + 16 * NREST)
                    for h in range(HP):
                        last = pe.matmul(M[0][:, 0:D], oT[:, h, :],
                                         wo[:, bass.ds(layer(f) % 2, 1), h, :].squeeze(1),
                                         start=(h == 0), stop=(h == HP - 1))
                    last.then_inc(wo_done, 1)

                def turn_y1():
                    wait(pe, y1_set, f, 1, 1)
                    pe.transpose(M[0][:, 0:P], y1s[:, :], ident[:, :]).then_inc(y1_turned, 1)

                def turn_back():
                    wait(pe, fT_set, f, 2, 2)
                    pe.transpose(M[0][:, 0:P], fT[:, f.u * P:(f.u + 1) * P], ident[:, :]).then_inc(f_back, 1)

                def turn_xn():
                    wait(pe, xn_set, e, 1, 1)
                    wait(pe, xst_set, e.back(1), 2, 2)
                    pe.transpose(M[1][:, 0:P], xn[:, :], ident[:, :]).then_inc(xn_back, 1)

                def ffn_in(k):
                    if k == 0:
                        wait(pe, xnT_set, e, 1, 1)
                    else:
                        wait(pe, hb_set, e, 2, 1)
                    pe.matmul(M[1][:, 0:FI], xnT[:, :],
                              w1[:, bass.ds(layer(e) % 2, 1), (1 - k) * FI:(2 - k) * FI].squeeze(1),
                              start=True, stop=True).then_inc(h_done, 1)

                def turn_u():
                    wait(pe, hu_set, e, 1, 1)
                    for c, (f0, fn) in enumerate(FC):
                        last = pe.transpose(M[1][0:fn, c * P:(c + 1) * P], hu[:, f0:f0 + fn], ident[:, :])
                    last.then_inc(u_turned, 1)

                def ffn_out():
                    wait(pe, uT_set, e, 2, 2)
                    for c, (f0, fn) in enumerate(FC):
                        last = pe.matmul(M[1][:, 0:D], uT[0:fn, c, :],
                                         w2[0:fn, bass.ds(layer(e) % 2, 1), c, :].squeeze(1),
                                         start=(c == 0), stop=(c == len(FC) - 1))
                    last.then_inc(w2_done, 1)

                def turn_y2():
                    wait(pe, y2_set, e, 1, 1)
                    pe.transpose(M[1][:, 0:P], y2s[:, :], ident[:, :]).then_inc(y2_turned, 1)

                if t:
                    score(0)
                if p:
                    project_qk(0)
                if e:
                    turn_xn()
                if f:
                    out_proj()
                if p:
                    project_qk(1)
                if t:
                    score(1)
                if e:
                    ffn_in(0)
                if p:
                    project_qk(2)
                if v:
                    weigh_tails()
                if f:
                    turn_y1()
                if p:
                    project_qk(3)
                if e:
                    ffn_in(1)
                if f:
                    turn_back()
                if n:
                    turn(0)
                if n:
                    turn(1)
                if v:
                    weigh()
                if n:
                    turn(2)
                if n:
                    turn(3)
                if e:
                    turn_u()
                if n:
                    project_v(0)
                if n:
                    project_v(1)
                if e:
                    ffn_out()
                if e:
                    turn_y2()

            run(pe, step)

        @block.vector
        def _(dve):
            dve.memset(mhalf[:, :], -0.5).then_inc(zero_set, 1)
            dve.memset(xst[:, :, 0:1], 0.0).then_inc(zero_set, 1)
            dve.memset(fT[:, 0:1], 0.0).then_inc(zero_set, 1)
            dve.memset(kT[:, 0, :, 0:WIN], 0.0).then_inc(zero_set, 1)

            def norm16(k, src, dst):
                for i in range(NT):
                    if k == 0 and i % UN == 0:
                        dve.wait_ge(x_in[i // UN], 16)
                    if k == 1 and i % UN == 0:
                        dve.wait_ge(x1_set, i // UN + 1)
                    dve.bn_stats(st16[:, i, :], src[:, i, :]).then_inc(xs_stat, 1)
                for i in range(NT):
                    dve.wait_ge(xs_stat, NT * k + i + 1)
                    dve.bn_aggr(mv16[:, i, :], st16[:, i, :]).then_inc(xs_aggr, 1)
                dve.wait_ge(xs_aggr, NT * (k + 1))
                dve.tensor_scalar(ve16[:, :], mv16[:, :, 1], 1e-5, None, ALU.add).then_inc(xs_ve, 1)
                dve.wait_ge(xs_rstd, k + 1)
                for i in range(NT):
                    dve.tensor_scalar(dst[:, i, :], src[:, i, :], mv16[:, i, 0:1], rs16[:, i:i + 1],
                                      ALU.subtract, ALU.mult).then_inc(xs_norm, 1)

            norm16(0, x1, xn16)
            dve.wait_ge(xw_in, 16 * 9)
            dve.wait_ge(xkv, 1)
            dve.tensor_tensor(vx, S[0][:, 0:P], bvb, ALU.add).then_inc(xv_set, 1)
            dve.wait_ge(const_in, 32)
            dve.tensor_copy(identb[:, :], ident[:, :]).then_inc(const_set, 1)
            for m in range(2):
                dve.tensor_copy(maskb[:, m, :, :], maskf[:, m, :].unsqueeze(1).to_broadcast([P, HP, 2 * WIN]))\
                    .then_inc(const_set, 1)
            sc = S[1][:, :].rearrange("p (a s) -> p a s", s=NS)
            e3 = ex0.rearrange("p (a s) -> p a s", s=NS)
            dve.wait_ge(xsc, 1)
            dve.tensor_reduce(smax[:, 0:NT], sc, AX.X, ALU.max).then_inc(xmax, 1)
            dve.wait_ge(xmax, 1)
            dve.tensor_tensor(e3, sc, smax[:, 0:NT].unsqueeze(2).to_broadcast([P, NT, NS]), ALU.subtract)\
                .then_inc(xsub, 1)
            dve.wait_ge(xexp, 1)
            dve.tensor_reduce(ssum[:, 0:NT], e3, AX.X, ALU.add).then_inc(xsum, 1)
            dve.wait_ge(xsum, 1)
            dve.reciprocal(rsum[:, 0:NT], ssum[:, 0:NT]).then_inc(xrec, 1)
            dve.wait_ge(xrec, 1)
            dve.tensor_tensor(px.rearrange("p (a s) -> p a s", s=NS), e3,
                              rsum[:, 0:NT].unsqueeze(2).to_broadcast([P, NT, NS]), ALU.mult).then_inc(xp, 1)
            dve.wait_ge(gate_set, 1)
            for b in range(B):
                dve.wait_ge(xatt, b + 1)
                xb = x1[:, b * UN:(b + 1) * UN, :].rearrange("p t d -> p (t d)")
                dve.scalar_tensor_tensor(xb, (X + O)[b][:, :], tgate[:, 0:1], xb, ALU.mult, ALU.add)\
                    .then_inc(x1_set, 1)
            norm16(1, x1, y)

            def step(at, live):
                r, t, v, f, e = (lagged(at, k) for k in (1, 3, 4, 5, 6))

                def norm():
                    wait(dve, rstd_set, e, 1, 1)
                    wait(dve, xn_back, e.back(1), 1, 1)
                    dve.tensor_scalar(xn[:, :], M[0][:, 0:D], mv[:, 0:1], rstd[:, 0:1],
                                      ALU.subtract, ALU.mult).then_inc(xn_set, 1)

                def turn_p():
                    dve.wait_ge(pT_zero, 1)
                    wait(dve, p_set, v, 1, 1)
                    wait(dve, weighed, v.back(1), 4, 4)
                    for w in range(QW):
                        for o in range(2):
                            q = (w - o) % QW
                            dve.transpose(pT[q * WIN:(q + 1) * WIN, :, w * WIN:(w + 1) * WIN],
                                          pn[w * WIN:(w + 1) * WIN, :, (1 - o) * WIN:(2 - o) * WIN])\
                                .then_inc(pT_set, 1)

                def row_max(k):
                    wait(dve, scored, t, 2, k + 1)
                    dve.tensor_reduce(smax[:, k * HP:(k + 1) * HP],
                                      S[k][:, :].rearrange("p (h j) -> p h j", h=HP), AX.X, ALU.max)\
                        .then_inc(max_set, 1)

                def subtract_max(k):
                    wait(dve, max_set, t, 2, k + 1)
                    if k == 0:
                        wait(dve, p_set, t.back(1), 1, 1)
                    dve.tensor_tensor(ex[:, k * HP:(k + 1) * HP, :],
                                      S[k][:, :].rearrange("p (h j) -> p h j", h=HP),
                                      smax[:, k * HP:(k + 1) * HP].unsqueeze(2)
                                      .to_broadcast([P, HP, 2 * WIN]), ALU.subtract).then_inc(less_max, 1)

                def sum_squares(k):
                    rp = r.u % 2
                    wait(dve, squared, r, 2, k + 1)
                    if k == 0:
                        wait(dve, rn_set, r.back(2), 1, 1)
                    dve.tensor_reduce(ss[:, rp, k * H:(k + 1) * H],
                                      sq[:, k * INNER:(k + 1) * INNER].rearrange("p (h d) -> p h d", d=DH),
                                      AX.X, ALU.add).then_inc(ss_set, 1)
                    if k == 1:
                        wait(dve, ss_set, r, 3, 2)
                        dve.tensor_scalar(ss[:, rp, :], ss[:, rp, :], 1e-24, None, ALU.max).then_inc(ss_set, 1)

                t14 = t1[:, :].rearrange("p (a h d) -> p a h d", a=2, h=H)
                t24 = t2[:, :].rearrange("p (a h d) -> p a h d", a=2, h=H)

                def q4():
                    return qk[:, r.u % 2, :].rearrange("p (a h d) -> p a h d", a=2, h=H)

                def table(kind, d0, dn):
                    tb = tab[:, bass.ds(layer(r), 1), r.u, kind:kind + 2, d0:d0 + dn].squeeze(1)
                    return tb.unsqueeze(2).to_broadcast([P, 2, H, dn])

                def rope_cos():
                    wait(dve, qk_copied, r, 4, 4)
                    wait(dve, qkr_set, r.back(1), 2, 2)
                    dve.tensor_tensor(t14, q4(), table(0, 0, DH), ALU.mult).then_inc(roped, 1)

                def rope_sin(k):
                    o = (1 - k) * HALF
                    wait(dve, rope_sum, r.back(1), 2, 2)
                    dve.tensor_tensor(t24[:, :, :, k * HALF:(k + 1) * HALF], q4()[:, :, :, o:o + HALF],
                                      table(2, k * HALF, HALF), ALU.mult).then_inc(roped, 1)

                def sum_exp():
                    wait(dve, exp_set, t, 1, 1)
                    dve.tensor_reduce(ssum[:, :], ex[:, :, :], AX.X, ALU.add).then_inc(sum_set, 1)
                    wait(dve, sum_set, t, 1, 1)
                    wait(dve, p_set, t.back(1), 1, 1)
                    dve.reciprocal(rsum[:, :], ssum[:, :]).then_inc(rsum_set, 1)

                def add_y1():
                    wait(dve, wo_done, f, 1, 1)
                    wait(dve, y1b_set, f.back(1), 1, 1)
                    yt = y[:, bass.ds(row(f) * UN + f.u, 1), :].squeeze(1)
                    dve.tensor_tensor(y1s[:, :], M[0][:, 0:D], yt, ALU.add).then_inc(y1_set, 1)

                def stats():
                    wait(dve, f_back, f, 1, 1)
                    dve.bn_stats(st[:, :], M[0][:, 0:D]).then_inc(st_set, 1)
                    dve.wait_ge(zero_set, 4)
                    wait(dve, st_set, f, 1, 1)
                    dve.bn_aggr(mv[:, :], st[:, :]).then_inc(mv_set, 1)
                    wait(dve, mv_set, f, 1, 1)
                    wait(dve, rstd_set, f.back(1), 1, 1)
                    dve.tensor_scalar(ve[:, :], mv[:, 1:2], 1e-5, None, ALU.add).then_inc(ve_set, 1)

                def add_b1(k):
                    wait(dve, h_done, e, 2, k + 1)
                    dst = ha if k else hg
                    dve.tensor_tensor(dst[:, :], M[1][:, 0:FI],
                                      b1b[:, bass.ds(layer(e) % 2, 1), (1 - k) * FI:(2 - k) * FI].squeeze(1),
                                      ALU.add).then_inc(hb_set, 1)

                def gate_u():
                    wait(dve, gelu_set, e, 1, 1)
                    wait(dve, hb_set, e, 2, 2)
                    dve.tensor_tensor(hu[:, :], ha[:, :], hg[:, :], ALU.mult).then_inc(hu_set, 1)

                def add_y2():
                    wait(dve, w2_done, e, 1, 1)
                    wait(dve, y1b_set, e, 1, 1)
                    wait(dve, y_kept, e.back(1), 1, 1)
                    dve.tensor_tensor(y2s[:, :], M[1][:, 0:D], y1b[:, e.u % 2, :], ALU.add).then_inc(y2_set, 1)

                if e:
                    norm()
                if v:
                    turn_p()
                if t:
                    row_max(0)
                    subtract_max(0)
                if r:
                    sum_squares(0)
                if f:
                    add_y1()
                if t:
                    row_max(1)
                    subtract_max(1)
                if r:
                    sum_squares(1)
                if e:
                    add_b1(0)
                if t:
                    sum_exp()
                if r:
                    if isinstance(r.g, int) and r.g == 0 and r.u == 0:
                        dve.wait_ge(tab_set, 6 * L)
                    rope_cos()
                if e:
                    add_b1(1)
                    gate_u()
                if r:
                    rope_sin(0)
                    rope_sin(1)
                if f:
                    stats()
                if e:
                    add_y2()

            run(dve, step)
            for b in range(B):
                dve.wait_ge(y_kept, G * UN - (B - 1 - b) * UN)
                xb = x1[:, b * UN:(b + 1) * UN, :].rearrange("p t d -> p (t d)")
                dve.scalar_tensor_tensor(xb, y[:, b * UN:(b + 1) * UN, :].rearrange("p t d -> p (t d)"),
                                         tgate[:, 1:2], xb, ALU.mult, ALU.add).then_inc(x1_set, 1)

        @block.gpsimd
        def _(pool):
            pool.memset(kT[:, 1, :, 0:WIN], 0.0).then_inc(const_set, 1)
            pool.memset(pT[:, :, :], 0.0).then_inc(pT_zero, 1)
            pool.wait_ge(zero_set, 1)
            pool.wait_ge(xs_ve, 1)
            pool.tensor_tensor(rs16[:, :], ve16[:, :], mhalf[:, 0:NT], ALU.pow).then_inc(xs_rstd, 1)
            pool.wait_ge(rope_in, 16 * 5)

            def scale_tables(l):
                for a in range(2):
                    pool.tensor_tensor(tab[:, l, :, a, :], ropeb[:, :, a, :],
                                       qks[:, a, l, :].unsqueeze(1).to_broadcast([P, UN, DH]), ALU.mult)\
                        .then_inc(tab_set, 1)
                    for n in range(2):
                        o = (1 - n) * HALF
                        pool.tensor_tensor(tab[:, l, :, 2 + a, n * HALF:(n + 1) * HALF],
                                           ropeb[:, :, 2 + a, n * HALF:(n + 1) * HALF],
                                           qks[:, a, l, o:o + HALF].unsqueeze(1).to_broadcast([P, UN, HALF]),
                                           ALU.mult).then_inc(tab_set, 1)

            for l in range(L):
                if l == 3:
                    pool.wait_ge(xs_ve, 2)
                    pool.tensor_tensor(rs16[:, :], ve16[:, :], mhalf[:, 0:NT], ALU.pow).then_inc(xs_rstd, 1)
                scale_tables(l)

            def step(at, live):
                r, n, t, f = (lagged(at, k) for k in (1, 2, 3, 5))
                if n:
                    wait(pool, roped, n, 3, 3)
                    for k in range(2):
                        pool.tensor_tensor(t1[:, k * INNER:(k + 1) * INNER], t1[:, k * INNER:(k + 1) * INNER],
                                           t2[:, k * INNER:(k + 1) * INNER], ALU.add).then_inc(rope_sum, 1)
                    wait(pool, rn_set, n, 1, 1)
                    wait(pool, turned, n.back(1), 4, 4)
                    for k in range(2):
                        wait(pool, rope_sum, n, 2, k + 1)
                        pool.tensor_tensor(qkr[:, k * INNER:(k + 1) * INNER].rearrange("p (a d) -> p a d", d=DH),
                                           t1[:, k * INNER:(k + 1) * INNER].rearrange("p (a d) -> p a d", d=DH),
                                           rn[:, n.u % 2, k * H:(k + 1) * H].unsqueeze(2)
                                           .to_broadcast([P, H, DH]), ALU.mult).then_inc(qkr_set, 1)
                if f:
                    pool.wait_ge(wrest_in, 16 * NREST)
                    wait(pool, y1_set, f, 1, 1)
                    wait(pool, y2_set, f.back(2), 1, 1)
                    pool.tensor_tensor(y1b[:, f.u % 2, :], y1s[:, :],
                                       b2b[:, bass.ds(layer(f) % 2, 1), :].squeeze(1), ALU.add).then_inc(y1b_set, 1)
                if t:
                    wait(pool, rsum_set, t, 1, 1)
                    wait(pool, pT_set, t.back(1), 8, 8)
                    pool.tensor_tensor(pn[:, :, :], ex[:, :, :],
                                       rsum[:, :].unsqueeze(2).to_broadcast([P, H, 2 * WIN]), ALU.mult)\
                        .then_inc(p_set, 1)
                if r:
                    wait(pool, ss_set, r, 3, 3)
                    wait(pool, qkr_set, r.back(2), 2, 2)
                    pool.tensor_tensor(rn[:, r.u % 2, :], ss[:, r.u % 2, :], mhalf[:, :], ALU.pow).then_inc(rn_set, 1)
                if f:
                    wait(pool, ve_set, f, 1, 1)
                    wait(pool, xn_set, f.back(1), 1, 1)
                    pool.tensor_tensor(rstd[:, :], ve[:, :], mhalf[:, 0:1], ALU.pow).then_inc(rstd_set, 1)

            run(pool, step)


_INS = ["x", "ctx_1024", "g_xattn", "g_ffn", "L0_xattn_Wq", "L0_xattn_bq", "L0_xattn_Wk", "L0_xattn_bk",
        "L0_xattn_Wv", "L0_xattn_bv", "L0_ffn_Wqkv", "L0_ffn_q_scale", "L0_ffn_k_scale", "L0_ffn_Wo",
        "L0_ffn_ln_g", "L0_ffn_ln_b", "L0_ffn_W1", "L0_ffn_b1", "L0_ffn_W2", "L0_ffn_b2"]


def _constants(n, dh):
    import numpy as np

    f = np.float32
    half = np.arange(0, dh, 2, dtype=f)
    inv_freq = (f(1.0) / f(10000.0) ** (half / f(dh))).astype(f)
    t = np.arange(n, dtype=f)
    freqs = (t[:, None] * inv_freq[None, :]).astype(f)
    base = ((half + f(0.4 * dh)) / f(1.4 * dh)).astype(f)
    scale = (base[None, :] ** ((t - n // 2) / f(WIN // 2))[:, None]).astype(f)
    cos, sin = np.cos(freqs), np.sin(freqs)
    inv = f(1.0) / scale
    kinds = [np.concatenate([a * m, b * m], -1) for a, b, m in
             ((cos, cos, scale * f(8.0)), (cos, cos, inv), (-sin, sin, scale * f(8.0)), (-sin, sin, inv))]
    rope = np.stack(kinds, 1).reshape(n // P, P, 4, dh).transpose(1, 0, 2, 3)
    i = (np.arange(P) % WIN)[:, None]
    j = np.arange(WIN)[None, :]
    low = f(-3.0e38)
    own = np.where(j > i, low, f(0))
    before = np.where(j < i, low, f(0))
    first = np.where((np.arange(P) < WIN)[:, None], low, before)
    masks = np.stack([np.concatenate([first, own], 1), np.concatenate([before, own], 1)], 1)
    return [np.ascontiguousarray(a, dtype=f) for a in (rope, masks, np.eye(P))]


def kernel(**inputs):
    import numpy as _np
    import concourse.bacc as _bacc
    from concourse import mybir as _mybir
    from concourse.bass_utils import run_bass_kernel_spmd as _run

    nc = _bacc.Bacc("TRN2", target_bir_lowering=False, num_devices=1)
    arrays, args = {}, []
    named = [(n, inputs[n]) for n in _INS]
    named += list(zip(("rope", "masks", "ident"), _constants(inputs["x"].shape[1], inputs["L0_ffn_q_scale"].shape[1])))
    for name, a in named:
        if name in ("L0_ffn_ln_g", "L0_ffn_ln_b"):
            a = _np.asarray(a).T
        a = _np.ascontiguousarray(a)
        arrays[f"in_{name}_dram"] = a
        args.append(nc.dram_tensor(f"in_{name}_dram", a.shape, _mybir.dt.from_np(a.dtype), kind="ExternalInput").ap())
    args.append(nc.dram_tensor("out_dram", inputs["x"].shape, _mybir.dt.float32, kind="ExternalOutput").ap())
    build(nc, *args)
    return _run(nc, [arrays], core_ids=[0]).results[0]["out_dram"]
```

```python
from contextlib import ExitStack

import concourse.bass as bass
from concourse import mybir

ALU = mybir.AluOpType
ACT = mybir.ActivationFunctionType
AX = mybir.AxisListType
F32 = mybir.dt.float32
BF16 = mybir.dt.bfloat16

P = 128
WIN = 32
QW = P // WIN
UN = 4


class Pos:

    def __init__(self, g, u):
        self.g, self.u = g, u

    def back(self, lag):
        d = (lag - self.u + UN - 1) // UN if lag > self.u else 0
        if isinstance(self.g, int) and self.g - d < 0:
            return None
        return Pos(self.g - d if d else self.g, self.u - lag + UN * d)

    def count(self, per, k):
        return self.g * (UN * per) + (self.u * per + k) if not isinstance(self.g, int) \
            else (self.g * UN + self.u) * per + k


def build(nc, x, ctx_in, g_xattn, g_ffn, Wq, bq, Wk, bk, Wv, bv, Wqkv, q_scale, k_scale, Wo, ln_g, ln_b,
          W1, b1, W2, b2, rope, masks, ident_in, out):
    B, N, D = x.shape
    NS = ctx_in.shape[1]
    L = Wqkv.shape[0]
    INNER = Wo.shape[1]
    DH = q_scale.shape[1]
    H = INNER // DH
    HP = H // 2
    HALF = DH // 2
    FI = W2.shape[1]
    FC = [(c, min(P, FI - c)) for c in range(0, FI, P)]
    NT = B * N // P
    G = L * B
    assert N == UN * P and D == P and B * NS == P and H * DH == 2 * 512 and NS == WIN
    NREST = 4 + len(FC)
    GL = 2

    with ExitStack() as ctx:
        def sb(name, shape, dt=F32):
            return ctx.enter_context(nc.sbuf_tensor(name, shape, dt))

        def bank(name):
            return ctx.enter_context(nc.psum_tensor(name, [P, 512], F32))

        def sem(name):
            return ctx.enter_context(nc.semaphore(name))

        X = [bank("px0"), bank("px1")]
        S = [bank("ps0"), bank("ps1")]
        O = [bank("po0"), bank("po1")]
        M = [bank("pm0"), bank("pm1")]

        wqkv = sb("wqkv", [P, 2, 3 * INNER])
        wo = sb("wo", [P, 2, HP, D])
        w1 = sb("w1", [P, 2, 2 * FI])
        w2 = sb("w2", [P, 2, len(FC), D])
        b1b = sb("b1b", [P, 2, 2 * FI])
        b2b = sb("b2b", [P, 2, D])
        lng = sb("lng", [P, L])
        lnb = sb("lnb", [P, L])
        tab = sb("tab", [P, L, UN, 4, DH])
        maskb = sb("maskb", [P, 2, HP, 2 * WIN], BF16)
        ident = sb("ident", [P, P])
        identb = sb("identb", [P, P], BF16)
        mhalf = sb("mhalf", [P, 2 * H])
        y = sb("y", [P, NT, D])
        x1 = sb("x1", [P, NT, D])
        xst = sb("xst", [P, B, N + 1])
        xstage = sb("xstage", [P, UN, P])
        qk = sb("qk", [P, 2, 2 * INNER])
        vb = sb("vb", [P, UN, INNER])
        sq = sb("sq", [P, 2 * INNER])
        t1 = sb("t1", [P, 2 * INNER])
        t2 = sb("t2", [P, 2 * INNER])
        qkr = sb("qkr", [P, 2 * INNER])
        ss = sb("ss", [P, 2, 2 * H])
        rn = sb("rn", [P, 2, 2 * H])
        qT = sb("qT", [P, 2, HP, P])
        kT = sb("kT", [P, 2, HP, WIN + P])
        smax = sb("smax", [P, H])
        ex = sb("ex", [P, H, 2 * WIN])
        ssum = sb("ssum", [P, H])
        rsum = sb("rsum", [P, H])
        pT = sb("pT", [P, H, P])
        oT = sb("oT", [P, HP, P])
        y1s = sb("y1s", [P, D])
        y1b = sb("y1b", [P, 2, D])
        y2s = sb("y2s", [P, D])
        fT = sb("fT", [P, N + 1])
        st = sb("st", [P, 6])
        mv = sb("mv", [P, 2])
        ve = sb("ve", [P, 1])
        rstd = sb("rstd", [P, 1])
        xn = sb("xn", [P, D])
        xnT = sb("xnT", [P, P])
        ha = sb("ha", [P, FI])
        hg = sb("hg", [P, FI])
        hu = ha
        uT = sb("uT", [P, len(FC), P])
        gates = sb("gates", [P, 2])
        tgate = sb("tgate", [P, 2])
        bqk = sb("bqk", [P, 2])
        ropeb = ex[:, :, :].rearrange("p h j -> p (h j)").rearrange("p (u k d) -> p u k d", u=UN, k=4)
        qks = oT[:, 0:2 * L * DH // P, :].rearrange("p h t -> p (h t)").rearrange("p (a l d) -> p a l d", a=2, l=L)
        maskf = oT[:, HP - 1, :].rearrange("p (m j) -> p m j", m=2)
        early = sq[:, 0:10 * NT]
        st16 = early[:, 0:6 * NT].rearrange("p (t k) -> p t k", k=6)
        mv16 = early[:, 6 * NT:8 * NT].rearrange("p (t k) -> p t k", k=2)
        ve16 = early[:, 8 * NT:9 * NT]
        rs16 = early[:, 9 * NT:10 * NT]
        xn16 = t1[:, :].rearrange("p (t d) -> p t d", d=D)
        xnT16 = t2[:, :]
        qTx = qkr[:, :]
        wx = qk[:, 0, 0:3 * P].rearrange("p (a d) -> p a d", a=3)
        cx = qk[:, 0, 3 * P:4 * P]
        wxT = qk[:, 0, 4 * P:8 * P]
        kTx = qk[:, 0, 8 * P:9 * P]
        vx = qk[:, 0, 9 * P:10 * P]
        bvb = qk[:, 0, 10 * P:11 * P]
        ex0 = qk[:, 1, 0:512]
        px = qk[:, 1, 512:1024]
        pxT = qk[:, 1, 1024:1536]

        x_in = [sem(f"x_in{b}") for b in range(B)]
        xw_in, const_in, rope_in = sem("xw_in"), sem("const_in"), sem("rope_in")
        wqkv_in, wrest_in = sem("wqkv_in"), sem("wrest_in")
        stored = sem("stored")
        const_set, zero_set, tab_set = sem("const_set"), sem("zero_set"), sem("tab_set")
        xs_stat, xs_aggr, xs_ve, xs_rstd, xs_norm = (sem(n) for n in
                                                     ("xs_stat", "xs_aggr", "xs_ve", "xs_rstd", "xs_norm"))
        xw_turned, xw_copied, xkv, xk_set, xv_set = (sem(n) for n in
                                                     ("xw_turned", "xw_copied", "xkv", "xk_set", "xv_set"))
        xn_turned, xn_copied, xq, xq_set, xsc = (sem(n) for n in ("xn_turned", "xn_copied", "xq", "xq_set", "xsc"))
        xmax, xsub, xexp, xsum, xrec, xp = (sem(n) for n in ("xmax", "xsub", "xexp", "xsum", "xrec", "xp"))
        xp_turned, xp_copied, xatt, gate_set, x1_set = (sem(n) for n in
                                                        ("xp_turned", "xp_copied", "xatt", "gate_set", "x1_set"))
        y0_turned, y0_copied = sem("y0_turned"), sem("y0_copied")
        staged = sem("staged")
        qk_done = sem("qk_done")
        qk_copied = sem("qk_copied")
        v_done = sem("v_done")
        v_copied = sem("v_copied")
        squared = sem("squared")
        ss_set = sem("ss_set")
        rn_set = sem("rn_set")
        roped = sem("roped")
        roped_k = sem("roped_k")
        rope_sum = sem("rope_sum")
        qkr_set = sem("qkr_set")
        turned = sem("turned")
        turned_copied = sem("turned_copied")
        scored = sem("scored")
        max_set = sem("max_set")
        less_max = sem("less_max")
        exp_set = sem("exp_set")
        sum_set = sem("sum_set")
        rsum_set = sem("rsum_set")
        p_set = sem("p_set")
        pT_zero = sem("pT_zero")
        pT_set = sem("pT_set")
        edge_done = sem("edge_done")
        weighed = sem("weighed")
        oT_set = sem("oT_set")
        wo_done = sem("wo_done")
        y1_set = sem("y1_set")
        y1b_set = sem("y1b_set")
        y1_turned = sem("y1_turned")
        fT_set = sem("fT_set")
        f_back = sem("f_back")
        st_set, mv_set, ve_set = sem("st_set"), sem("mv_set"), sem("ve_set")
        rstd_set = sem("rstd_set")
        xn_set = sem("xn_set")
        xn_back = sem("xn_back")
        xnT_set = sem("xnT_set")
        h_done = sem("h_done")
        hb_set = sem("hb_set")
        gelu_set = sem("gelu_set")
        hu_set = sem("hu_set")
        u_turned = sem("u_turned")
        uT_set = sem("uT_set")
        w2_done = sem("w2_done")
        y2_set = sem("y2_set")
        y_kept = sem("y_kept")
        y2_turned = sem("y2_turned")
        xst_set = sem("xst_set")

        def wait(eng, s, at, per, k):
            if at is not None:
                eng.wait_ge(s, at.count(per, k))

        def layer(at):
            return at.g // B

        def row(at):
            return at.g % B

        LAST = 7

        def run(eng, step):
            for g in range(GL):
                for u in range(UN):
                    step(Pos(g, u))
            with eng.Fori(GL, G) as g:
                for u in range(UN):
                    step(Pos(g, u))
            for k in range(LAST):
                step(Pos(G + k // UN, k % UN))

        def lagged(at, lag):
            p = at.back(lag)
            return p if p is None or not isinstance(p.g, int) or p.g < G else None

        def do(at, lag, stage, *args):
            tile = lagged(at, lag)
            if tile is not None:
                stage(tile, *args)

        block = ctx.enter_context(nc.Block())

        @block.sync
        def _(sp):
            sp.dma_start(ident[:, :], ident_in).then_inc(const_in, 16)
            for b in range(B):
                sp.dma_start(x1[:, b * UN:(b + 1) * UN, :],
                             x[b].rearrange("(t p) d -> p t d", p=P)).then_inc(x_in[b], 16)
            for a, w in enumerate((Wq, Wk, Wv)):
                sp.dma_start(wx[:, a, :], w).then_inc(xw_in, 16)
            sp.dma_start(cx, ctx_in.rearrange("b s d -> (b s) d")).then_inc(xw_in, 16)
            sp.dma_start(bvb, bv.partition_broadcast(P)).then_inc(xw_in, 16)
            sp.dma_start(bqk[:, 0:1], bq.unsqueeze(1)).then_inc(xw_in, 16)
            sp.dma_start(bqk[:, 1:2], bk.unsqueeze(1)).then_inc(xw_in, 16)
            sp.dma_start(gates[:, 0:1], g_xattn.partition_broadcast(P)).then_inc(xw_in, 16)
            sp.dma_start(gates[:, 1:2], g_ffn.partition_broadcast(P)).then_inc(xw_in, 16)
            sp.dma_start(maskf[:, :, :], masks).then_inc(const_in, 16)
            sp.dma_start(ropeb[:, :, :, :], rope).then_inc(rope_in, 16)
            sp.dma_start(qks[:, 0, :, :], q_scale.partition_broadcast(P)).then_inc(rope_in, 16)
            sp.dma_start(qks[:, 1, :, :], k_scale.partition_broadcast(P)).then_inc(rope_in, 16)
            sp.dma_start(lng[:, :], ln_g).then_inc(rope_in, 16)
            sp.dma_start(lnb[:, :], ln_b).then_inc(rope_in, 16)

            for l in range(L):
                h = l % 2
                if l >= 1:
                    sp.wait_ge(wqkv_in, 16 * l)
                    sp.wait_ge(wrest_in, 16 * NREST * l)
                if l >= 2:
                    sp.wait_ge(y2_set, NT * (l - 1))
                sp.dma_start(wqkv[:, h, :], Wqkv[l]).then_inc(wqkv_in, 16)
                sp.dma_start(wo[:, h, :, :], Wo[l].rearrange("(h p) d -> p h d", p=P)).then_inc(wrest_in, 16)
                sp.dma_start(w1[:, h, :], W1[l]).then_inc(wrest_in, 16)
                for c, (f0, fn) in enumerate(FC):
                    sp.dma_start(w2[0:fn, h, c, :], W2[l, f0:f0 + fn, :]).then_inc(wrest_in, 16)
                sp.dma_start(b1b[:, h, :], b1[l].partition_broadcast(P)).then_inc(wrest_in, 16)
                sp.dma_start(b2b[:, h, :], b2[l].partition_broadcast(P)).then_inc(wrest_in, 16)
            for b in range(B):
                sp.wait_ge(x1_set, B + b + 1)
                sp.dma_start(out[b].rearrange("(t p) d -> p t d", p=P),
                             x1[:, b * UN:(b + 1) * UN, :]).then_inc(stored, 16)
            sp.wait_ge(stored, 16 * B)

        @block.scalar
        def _(act):
            act.wait_ge(xw_in, 16 * 9)
            act.activation(tgate[:, :], gates[:, :], ACT.Tanh).then_inc(gate_set, 1)
            act.wait_ge(xw_turned, 1)
            act.copy(wxT, M[0][:, :]).then_inc(xw_copied, 1)
            act.wait_ge(xkv, 1)
            act.activation(kTx, M[1][:, 0:P], ACT.Identity, bias=bqk[:, 1:2]).then_inc(xk_set, 1)
            for b in range(B):
                act.wait_ge(xn_turned, b + 1)
                act.copy(xnT16[:, b * N:(b + 1) * N], (X + O)[b][:, :]).then_inc(xn_copied, 1)
            for b in range(B):
                act.wait_ge(xq, b + 1)
                act.activation(qTx[:, b * N:(b + 1) * N], (X + O)[b][:, :], ACT.Identity,
                               bias=bqk[:, 0:1]).then_inc(xq_set, 1)
            act.wait_ge(xsub, 1)
            act.activation(ex0, ex0, ACT.Exp).then_inc(xexp, 1)
            act.wait_ge(xp_turned, 1)
            act.copy(pxT, M[0][:, :]).then_inc(xp_copied, 1)
            act.wait_ge(zero_set, 4)
            for b in range(B):
                act.wait_ge(y0_turned, b + 1)
                act.copy(xst[0:64, b, 0:N], (X + O)[b][0:64, :]).then_inc(y0_copied, 1)
                act.copy(xst[64:P, b, 1:N + 1], (X + O)[b][64:P, :]).then_inc(y0_copied, 1)
            act.wait_ge(y0_copied, 2)
            act.copy(xstage[:, 0, :], xst[:, 0, 0:P]).then_inc(staged, 1)

            def step(at):
                def copy_weighed(f, k):
                    wait(act, weighed, f, 4, 2 * k + 2)
                    wait(act, wo_done, f.back(1), 1, 1)
                    act.copy(oT[:, 4 * k:4 * k + 4, :],
                             O[k][:, :].rearrange("p (h t) -> p h t", h=4)).then_inc(oT_set, 1)

                def square(p, k):
                    wait(act, qk_copied, p, 4, 2 * k + 2)
                    wait(act, ss_set, p.back(1), 3, 2)
                    act.activation(sq[:, k * INNER:(k + 1) * INNER], qk[:, p.u % 2, k * INNER:(k + 1) * INNER],
                                   ACT.Square).then_inc(squared, 1)

                def scale_xn(e):
                    l = layer(e)
                    act.wait_ge(rope_in, 16 * 5)
                    wait(act, xn_back, e, 1, 1)
                    act.activation(xnT[:, :], M[1][:, 0:P], ACT.Identity, scale=lng[:, bass.ds(l, 1)],
                                   bias=lnb[:, bass.ds(l, 1)]).then_inc(xnT_set, 1)

                def exps(t):
                    wait(act, less_max, t, 2, 2)
                    act.activation(ex[:, :, :], ex[:, :, :], ACT.Exp).then_inc(exp_set, 1)

                def copy_qk(p, c):
                    wait(act, qk_done, p, 4, c + 1)
                    if c == 0:
                        wait(act, roped, p.back(2), 3, 3)
                        wait(act, roped_k, p.back(2), 1, 1)
                    act.copy(qk[:, p.u % 2, c * 512:(c + 1) * 512], X[c % 2][:, :]).then_inc(qk_copied, 1)

                def shift_y1(f):
                    c0 = P * f.u
                    wait(act, y1_turned, f, 1, 1)
                    act.copy(fT[0:64, c0:c0 + P], M[0][0:64, 0:P]).then_inc(fT_set, 1)
                    act.copy(fT[64:P, c0 + 1:c0 + 1 + P], M[0][64:P, 0:P]).then_inc(fT_set, 1)

                def gelu(e):
                    wait(act, hb_set, e, 2, 1)
                    act.activation(hg[:, :], hg[:, :], ACT.Gelu).then_inc(gelu_set, 1)

                def copy_turned(n, k):
                    wait(act, turned, n, 4, k + 1)
                    if k == 0:
                        wait(act, scored, n.back(2), 2, 2)
                    src = X[k % 2][:, :].rearrange("p (h t) -> p h t", h=4)
                    dst = (qT[:, n.u % 2, 4 * k:4 * k + 4, :] if k < 2
                           else kT[:, n.u % 2, 4 * k - 8:4 * k - 4, WIN:WIN + P])
                    act.copy(dst, src).then_inc(turned_copied, 1)

                def carry_keys(n):
                    wait(act, turned_copied, n, 5, 4)
                    wait(act, scored, n.back(1), 2, 2)
                    act.copy(kT[:, 1 - n.u % 2, :, 0:WIN], kT[:, n.u % 2, :, P:P + WIN]).then_inc(turned_copied, 1)

                def copy_v(n, c):
                    wait(act, v_done, n, 2, c + 1)
                    if c == 0:
                        wait(act, weighed, n.back(3), 4, 4)
                    act.copy(vb[:, n.u, c * 512:(c + 1) * 512], X[c][:, :]).then_inc(v_copied, 1)

                def copy_u(e):
                    wait(act, u_turned, e, 1, 1)
                    nf = len(FC) - 1
                    act.copy(uT[:, 0:nf, :], M[1][:, 0:nf * P].rearrange("p (c t) -> p c t", c=nf)).then_inc(uT_set, 1)
                    act.copy(uT[0:FC[nf][1], nf, :], M[1][0:FC[nf][1], nf * P:(nf + 1) * P]).then_inc(uT_set, 1)

                def shift_y2(e):
                    c0 = P * e.u
                    wait(act, y2_turned, e, 1, 1)
                    b = row(e)
                    act.copy(xst[0:64, bass.ds(b, 1), c0:c0 + P].squeeze(1), M[1][0:64, 0:P]).then_inc(xst_set, 1)
                    act.copy(xst[64:P, bass.ds(b, 1), c0 + 1:c0 + 1 + P].squeeze(1),
                             M[1][64:P, 0:P]).then_inc(xst_set, 1)
                    act.copy(y[:, bass.ds(b * UN + e.u, 1), :].squeeze(1), y2s[:, :]).then_inc(y_kept, 1)

                def stage_next(p):
                    nxt = Pos(at.g, at.u + 1) if at.u + 1 < UN else Pos(at.g + 1, 0)
                    wait(act, xst_set, at.back(8), 2, 2)
                    wait(act, v_done, at.back(3), 2, 2)
                    act.copy(xstage[:, nxt.u, :],
                             xst[:, bass.ds(row(nxt), 1), nxt.u * P:nxt.u * P + P].squeeze(1)).then_inc(staged, 1)

                do(at, 3, copy_turned, 3)
                do(at, 7, gelu)
                do(at, 3, copy_v, 0)
                do(at, 5, copy_weighed, 0)
                do(at, 5, copy_weighed, 1)
                do(at, 3, copy_v, 1)
                do(at, 3, carry_keys)
                do(at, 7, copy_u)
                do(at, 1, square, 1)
                do(at, 5, shift_y1)
                do(at, 0, copy_qk, 0)
                do(at, 7, shift_y2)
                do(at, 0, copy_qk, 1)
                do(at, 0, stage_next)
                do(at, 0, square, 0)
                do(at, 6, scale_xn)
                do(at, 0, copy_qk, 2)
                do(at, 0, copy_qk, 3)
                do(at, 3, exps)
                do(at, 2, copy_turned, 0)
                do(at, 2, copy_turned, 1)
                do(at, 2, copy_turned, 2)

            run(act, step)

        @block.tensor
        def _(pe):
            pe.wait_ge(const_in, 32)
            pe.wait_ge(xw_in, 16 * 9)
            for a in range(4):
                last = pe.transpose(M[0][:, a * P:(a + 1) * P], wx[:, a, :] if a < 3 else cx, ident[:, :])
            last.then_inc(xw_turned, 1)
            pe.wait_ge(xw_copied, 1)
            ctxT = wxT[:, 3 * P:4 * P]
            pe.matmul(S[0][:, 0:P], ctxT, wxT[:, 2 * P:3 * P], start=True, stop=True)
            pe.matmul(M[1][:, 0:P], wxT[:, P:2 * P], ctxT, start=True, stop=True).then_inc(xkv, 1)
            for b in range(B):
                pe.wait_ge(xs_norm, UN * (b + 1))
                for u in range(UN):
                    last = pe.transpose((X + O)[b][:, u * P:(u + 1) * P], xn16[:, b * UN + u, :], ident[:, :])
                last.then_inc(xn_turned, 1)
            for b in range(B):
                pe.wait_ge(xn_copied, b + 1)
                pe.matmul((X + O)[b][:, :], wxT[:, 0:P], xnT16[:, b * N:(b + 1) * N], start=True, stop=True)\
                    .then_inc(xq, 1)
            pe.wait_ge(xk_set, 1)
            for b in range(B):
                pe.wait_ge(xq_set, b + 1)
                for u in range(UN):
                    c = (u * B + b) * NS
                    last = pe.matmul(S[1][:, c:c + NS], qTx[:, b * N + u * P:b * N + (u + 1) * P],
                                     kTx[:, b * NS:(b + 1) * NS], start=True, stop=True)
            last.then_inc(xsc, 1)
            pe.wait_ge(xp, 1)
            for u in range(UN):
                last = pe.transpose(M[0][:, u * P:(u + 1) * P], px[:, u * P:(u + 1) * P], ident[:, :])
            last.then_inc(xp_turned, 1)
            pe.wait_ge(xp_copied, 1)
            pe.wait_ge(xv_set, 1)
            for b in range(B):
                for u in range(UN):
                    last = pe.matmul((X + O)[b][:, u * P:(u + 1) * P],
                                     pxT[b * NS:(b + 1) * NS, u * P:(u + 1) * P],
                                     vx[b * NS:(b + 1) * NS, :], start=True, stop=True)
                last.then_inc(xatt, 1)
            for b in range(B):
                pe.wait_ge(x1_set, b + 1)
                pe.wait_ge(xs_norm, NT + UN * (b + 1))
                for u in range(UN):
                    last = pe.transpose((X + O)[b][:, u * P:(u + 1) * P], y[:, b * UN + u, :], ident[:, :])
                last.then_inc(y0_turned, 1)
            pe.wait_ge(y0_copied, 2 * B)
            pe.wait_ge(const_set, 4)

            def step(at):
                def project_qk(p, c):
                    if c == 0:
                        wait(pe, staged, p, 1, 1)
                        pe.wait_ge(wqkv_in, layer(p) * 16 + 16)
                    if c < 2:
                        wait(pe, qk_copied, p.back(1), 4, c + 3)
                        wait(pe, v_copied, p.back(3), 2, c + 1)
                    else:
                        wait(pe, qk_copied, p, 4, c - 1)
                    w = wqkv[:, bass.ds(layer(p) % 2, 1), c * 512:(c + 1) * 512].squeeze(1)
                    pe.matmul(X[c % 2][:, :], xstage[:, p.u, :], w, start=True, stop=True).then_inc(qk_done, 1)

                def turn(n, k):
                    if k == 0:
                        wait(pe, qkr_set, n, 2, 2)
                    if k >= 2:
                        wait(pe, turned_copied, n, 5, k - 1)
                    elif lagged(at, 0):
                        wait(pe, qk_copied, at, 4, k + 3)
                    else:
                        wait(pe, v_copied, n.back(1), 2, k + 1)
                    for j in range(4):
                        c = (4 * k + j) * P
                        last = pe.transpose(X[k % 2][:, j * P:(j + 1) * P], qkr[:, c:c + P], ident[:, :])
                    last.then_inc(turned, 1)

                def project_v(n, c):
                    wait(pe, turned_copied, n, 5, c + 3)
                    w = wqkv[:, bass.ds(layer(n) % 2, 1), 2 * INNER + c * 512:2 * INNER + (c + 1) * 512].squeeze(1)
                    pe.matmul(X[c][:, :], xstage[:, n.u, :], w, start=True, stop=True).then_inc(v_done, 1)

                def score(t, q):
                    tp = t.u % 2
                    if q == 0:
                        wait(pe, turned_copied, t, 5, 4)
                        wait(pe, turned_copied, t.back(1), 5, 5)
                    wait(pe, less_max, t.back(1), 2, q + 1)
                    pe.matmul(S[q][:, :], identb[:, :], maskb[:, 0 if t.u == 0 else 1, :, :],
                              start=True, stop=False, skip_group_check=True)
                    for h in range(HP):
                        for w in range(QW):
                            last = pe.matmul(S[q][w * WIN:(w + 1) * WIN, h * 2 * WIN:(h + 1) * 2 * WIN],
                                             qT[64 * q:64 * q + 64, tp, h, w * WIN:(w + 1) * WIN],
                                             kT[64 * q:64 * q + 64, tp, h, w * WIN:(w + 2) * WIN],
                                             start=False, stop=True, skip_group_check=True)
                    last.then_inc(scored, 1)

                def weigh_half(v, i, hq, first, edge):
                    par, hp = i % 2, 4 * (i // 2) + hq
                    out_ = O[i // 2][64 * par:64 * par + 64, hq * P:hq * P + (WIN if edge else P)]
                    ch = slice((2 * hp + par) * DH, (2 * hp + par + 1) * DH)
                    if edge:
                        vals, probs = vb[P - WIN:P, v.u - 1, ch], ex[P - WIN:P, par * HP + hp, 0:WIN]
                    else:
                        vals, probs = vb[:, v.u, ch], pT[:, par * HP + hp, :]
                    return pe.matmul(out_, vals, probs, start=first and hq == 0, stop=True, skip_group_check=True)

                def weigh_edge(v):
                    if v.u == 0:
                        return
                    wait(pe, pT_set, v, 8, 2)
                    wait(pe, oT_set, v.back(1), 2, 2)
                    for hq in range(4):
                        for i in range(4):
                            last = weigh_half(v, i, hq, True, True)
                            if hq == 3:
                                last.then_inc(edge_done, 1)

                def weigh(v):
                    wait(pe, pT_set, v, 8, 8)
                    wait(pe, v_copied, v, 2, 2)
                    wait(pe, oT_set, v.back(1), 2, 2)
                    for hq in range(4):
                        for i in range(4):
                            if hq == 0 and v.u:
                                pe.wait_ge(edge_done, v.g * (4 * UN - 4) + (4 * v.u - 3 + i))
                            last = weigh_half(v, i, hq, v.u == 0, False)
                            if hq == 3:
                                last.then_inc(weighed, 1)

                def out_proj(f):
                    wait(pe, oT_set, f, 2, 2)
                    wait(pe, xn_set, f.back(1), 1, 1)
                    pe.wait_ge(wrest_in, layer(f) * (16 * NREST) + 16 * NREST)
                    for h in range(HP):
                        last = pe.matmul(M[0][:, 0:D], oT[:, h, :],
                                         wo[:, bass.ds(layer(f) % 2, 1), h, :].squeeze(1),
                                         start=(h == 0), stop=(h == HP - 1))
                    last.then_inc(wo_done, 1)

                def turn_y1(f):
                    wait(pe, y1_set, f, 1, 1)
                    pe.transpose(M[0][:, 0:P], y1s[:, :], ident[:, :]).then_inc(y1_turned, 1)

                def turn_back(f):
                    wait(pe, fT_set, f, 2, 2)
                    pe.transpose(M[0][:, 0:P], fT[:, f.u * P:(f.u + 1) * P], ident[:, :]).then_inc(f_back, 1)

                def turn_xn(e):
                    wait(pe, xn_set, e, 1, 1)
                    wait(pe, xst_set, e.back(1), 2, 2)
                    pe.transpose(M[1][:, 0:P], xn[:, :], ident[:, :]).then_inc(xn_back, 1)

                def ffn_in(e, k):
                    if k == 0:
                        wait(pe, xnT_set, e, 1, 1)
                    else:
                        wait(pe, hb_set, e, 2, 1)
                    pe.matmul(M[1][:, 0:FI], xnT[:, :],
                              w1[:, bass.ds(layer(e) % 2, 1), (1 - k) * FI:(2 - k) * FI].squeeze(1),
                              start=True, stop=True).then_inc(h_done, 1)

                def turn_u(e):
                    wait(pe, hu_set, e, 1, 1)
                    for c, (f0, fn) in enumerate(FC):
                        last = pe.transpose(M[1][0:fn, c * P:(c + 1) * P], hu[:, f0:f0 + fn], ident[:, :])
                    last.then_inc(u_turned, 1)

                def ffn_out(e):
                    wait(pe, uT_set, e, 2, 2)
                    for c, (f0, fn) in enumerate(FC):
                        last = pe.matmul(M[1][:, 0:D], uT[0:fn, c, :],
                                         w2[0:fn, bass.ds(layer(e) % 2, 1), c, :].squeeze(1),
                                         start=(c == 0), stop=(c == len(FC) - 1))
                    last.then_inc(w2_done, 1)

                def turn_y2(e):
                    wait(pe, y2_set, e, 1, 1)
                    pe.transpose(M[1][:, 0:P], y2s[:, :], ident[:, :]).then_inc(y2_turned, 1)

                do(at, 3, score, 0)
                do(at, 7, turn_u)
                do(at, 5, out_proj)
                do(at, 7, ffn_out)
                do(at, 0, project_qk, 0)
                do(at, 5, turn_y1)
                do(at, 3, score, 1)
                do(at, 7, turn_y2)
                do(at, 0, project_qk, 1)
                do(at, 0, project_qk, 2)
                do(at, 4, weigh_edge)
                do(at, 6, turn_xn)
                do(at, 0, project_qk, 3)
                do(at, 5, turn_back)
                do(at, 6, ffn_in, 0)
                do(at, 2, turn, 0)
                do(at, 2, turn, 1)
                do(at, 4, weigh)
                do(at, 2, turn, 2)
                do(at, 2, turn, 3)
                do(at, 6, ffn_in, 1)
                do(at, 2, project_v, 0)
                do(at, 2, project_v, 1)

            run(pe, step)

        @block.vector
        def _(dve):
            dve.memset(mhalf[:, :], -0.5).then_inc(zero_set, 1)
            dve.memset(xst[:, :, 0:1], 0.0).then_inc(zero_set, 1)
            dve.memset(fT[:, 0:1], 0.0).then_inc(zero_set, 1)
            dve.memset(kT[:, 0, :, 0:WIN], 0.0).then_inc(zero_set, 1)

            def norm16(k, src, dst):
                for i in range(NT):
                    if k == 0 and i % UN == 0:
                        dve.wait_ge(x_in[i // UN], 16)
                    if k == 1 and i % UN == 0:
                        b = i // UN
                        if b == 0:
                            dve.wait_ge(gate_set, 1)
                        dve.wait_ge(xatt, b + 1)
                        xb = x1[:, b * UN:(b + 1) * UN, :].rearrange("p t d -> p (t d)")
                        dve.scalar_tensor_tensor(xb, (X + O)[b][:, :], tgate[:, 0:1], xb, ALU.mult, ALU.add)\
                            .then_inc(x1_set, 1)
                        dve.wait_ge(x1_set, b + 1)
                    dve.bn_stats(st16[:, i, :], src[:, i, :]).then_inc(xs_stat, 1)
                for i in range(NT):
                    dve.wait_ge(xs_stat, NT * k + i + 1)
                    dve.bn_aggr(mv16[:, i, :], st16[:, i, :]).then_inc(xs_aggr, 1)
                dve.wait_ge(xs_aggr, NT * (k + 1))
                dve.tensor_scalar(ve16[:, :], mv16[:, :, 1], 1e-5, None, ALU.add).then_inc(xs_ve, 1)
                dve.wait_ge(xs_rstd, k + 1)
                for i in range(NT):
                    dve.tensor_scalar(dst[:, i, :], src[:, i, :], mv16[:, i, 0:1], rs16[:, i:i + 1],
                                      ALU.subtract, ALU.mult).then_inc(xs_norm, 1)

            norm16(0, x1, xn16)
            dve.wait_ge(xw_in, 16 * 9)
            dve.wait_ge(xkv, 1)
            dve.tensor_tensor(vx, S[0][:, 0:P], bvb, ALU.add).then_inc(xv_set, 1)
            dve.wait_ge(const_in, 32)
            dve.tensor_copy(identb[:, :], ident[:, :]).then_inc(const_set, 1)
            for m in range(2):
                dve.tensor_copy(maskb[:, m, :, :], maskf[:, m, :].unsqueeze(1).to_broadcast([P, HP, 2 * WIN]))\
                    .then_inc(const_set, 1)
            sc = S[1][:, :].rearrange("p (a s) -> p a s", s=NS)
            e3 = ex0.rearrange("p (a s) -> p a s", s=NS)
            dve.wait_ge(xsc, 1)
            dve.tensor_reduce(smax[:, 0:NT], sc, AX.X, ALU.max).then_inc(xmax, 1)
            dve.wait_ge(xmax, 1)
            dve.tensor_tensor(e3, sc, smax[:, 0:NT].unsqueeze(2).to_broadcast([P, NT, NS]), ALU.subtract)\
                .then_inc(xsub, 1)
            dve.wait_ge(xexp, 1)
            dve.tensor_reduce(ssum[:, 0:NT], e3, AX.X, ALU.add).then_inc(xsum, 1)
            dve.wait_ge(xsum, 1)
            dve.reciprocal(rsum[:, 0:NT], ssum[:, 0:NT]).then_inc(xrec, 1)
            dve.wait_ge(xrec, 1)
            dve.tensor_tensor(px.rearrange("p (a s) -> p a s", s=NS), e3,
                              rsum[:, 0:NT].unsqueeze(2).to_broadcast([P, NT, NS]), ALU.mult).then_inc(xp, 1)
            norm16(1, x1, y)

            def step(at):
                def norm(e):
                    wait(dve, rstd_set, e, 1, 1)
                    wait(dve, xn_back, e.back(1), 1, 1)
                    dve.tensor_scalar(xn[:, :], M[0][:, 0:D], mv[:, 0:1], rstd[:, 0:1],
                                      ALU.subtract, ALU.mult).then_inc(xn_set, 1)

                def turn_block(v, w, before):
                    q = (w - before) % QW
                    src = ex[w * WIN:(w + 1) * WIN, :, (1 - before) * WIN:(2 - before) * WIN]
                    dst = ex[q * WIN:(q + 1) * WIN, :, 0:WIN] if q > w else \
                        pT[q * WIN:(q + 1) * WIN, :, w * WIN:(w + 1) * WIN]
                    dve.transpose(dst, src).then_inc(pT_set, 1)

                def turn_edge(v):
                    dve.wait_ge(pT_zero, 1)
                    wait(dve, p_set, v, 1, 1)
                    wait(dve, weighed, v.back(1), 4, 4)
                    turn_block(v, QW - 1, 1)
                    wait(dve, pT_set, v, 8, 1)
                    turn_block(v, 0, 1)

                def turn_rest(v):
                    for w in range(1, QW - 1):
                        turn_block(v, w, 1)
                    for w in range(QW):
                        turn_block(v, w, 0)

                def row_max(t, k):
                    wait(dve, scored, t, 2, k + 1)
                    dve.tensor_reduce(smax[:, k * HP:(k + 1) * HP],
                                      S[k][:, :].rearrange("p (h j) -> p h j", h=HP), AX.X, ALU.max)\
                        .then_inc(max_set, 1)

                def subtract_max(t, k):
                    wait(dve, max_set, t, 2, k + 1)
                    if k == 0:
                        last = t.back(1)
                        wait(dve, pT_set, last, 8, 8)
                        if last and last.u:
                            dve.wait_ge(edge_done, last.g * (4 * UN - 4) + 4 * last.u)
                    dve.tensor_tensor(ex[:, k * HP:(k + 1) * HP, :],
                                      S[k][:, :].rearrange("p (h j) -> p h j", h=HP),
                                      smax[:, k * HP:(k + 1) * HP].unsqueeze(2)
                                      .to_broadcast([P, HP, 2 * WIN]), ALU.subtract).then_inc(less_max, 1)

                def sum_squares(r, k):
                    rp = r.u % 2
                    wait(dve, squared, r, 2, k + 1)
                    if k == 0:
                        wait(dve, rn_set, r.back(2), 1, 1)
                    dve.tensor_reduce(ss[:, rp, k * H:(k + 1) * H],
                                      sq[:, k * INNER:(k + 1) * INNER].rearrange("p (h d) -> p h d", d=DH),
                                      AX.X, ALU.add).then_inc(ss_set, 1)
                    if k == 1:
                        wait(dve, ss_set, r, 3, 2)
                        dve.tensor_scalar(ss[:, rp, :], ss[:, rp, :], 1e-24, None, ALU.max).then_inc(ss_set, 1)

                t14 = t1[:, :].rearrange("p (a h d) -> p a h d", a=2, h=H)
                t24 = t2[:, :].rearrange("p (a h d) -> p a h d", a=2, h=H)

                def q4(r):
                    return qk[:, r.u % 2, :].rearrange("p (a h d) -> p a h d", a=2, h=H)

                def table(r, kind, d0, dn):
                    tb = tab[:, bass.ds(layer(r), 1), r.u, kind:kind + 2, d0:d0 + dn].squeeze(1)
                    return tb.unsqueeze(2).to_broadcast([P, 2, H, dn])

                def rope_cos(r):
                    if isinstance(r.g, int) and r.g == 0 and r.u == 0:
                        dve.wait_ge(tab_set, 6 * L)
                    wait(dve, qk_copied, r, 4, 4)
                    wait(dve, qkr_set, r.back(1), 2, 2)
                    dve.tensor_tensor(t14, q4(r), table(r, 0, 0, DH), ALU.mult).then_inc(roped, 1)

                def rope_sin(r, k):
                    o = (1 - k) * HALF
                    a = 2 - k
                    wait(dve, rope_sum, r.back(1), 2, 2)
                    dve.tensor_tensor(t24[:, 0:a, :, k * HALF:(k + 1) * HALF], q4(r)[:, 0:a, :, o:o + HALF],
                                      table(r, 2, k * HALF, HALF)[:, 0:a, :, :], ALU.mult).then_inc(roped, 1)

                def sum_exp(t):
                    wait(dve, exp_set, t, 1, 1)
                    dve.tensor_reduce(ssum[:, :], ex[:, :, :], AX.X, ALU.add).then_inc(sum_set, 1)

                def invert_sum(t):
                    wait(dve, sum_set, t, 1, 1)
                    wait(dve, p_set, t.back(1), 1, 1)
                    dve.reciprocal(rsum[:, :], ssum[:, :]).then_inc(rsum_set, 1)

                def add_y1(f):
                    wait(dve, wo_done, f, 1, 1)
                    wait(dve, y1b_set, f.back(1), 1, 1)
                    yt = y[:, bass.ds(row(f) * UN + f.u, 1), :].squeeze(1)
                    dve.tensor_tensor(y1s[:, :], M[0][:, 0:D], yt, ALU.add).then_inc(y1_set, 1)

                def stats(f):
                    wait(dve, f_back, f, 1, 1)
                    dve.bn_stats(st[:, :], M[0][:, 0:D]).then_inc(st_set, 1)

                def mean_var(f):
                    dve.wait_ge(zero_set, 4)
                    wait(dve, st_set, f, 1, 1)
                    dve.bn_aggr(mv[:, :], st[:, :]).then_inc(mv_set, 1)

                def add_eps(f):
                    wait(dve, mv_set, f, 1, 1)
                    wait(dve, rstd_set, f.back(1), 1, 1)
                    dve.tensor_scalar(ve[:, :], mv[:, 1:2], 1e-5, None, ALU.add).then_inc(ve_set, 1)

                def add_b1(e, k):
                    wait(dve, h_done, e, 2, k + 1)
                    dst = ha if k else hg
                    dve.tensor_tensor(dst[:, :], M[1][:, 0:FI],
                                      b1b[:, bass.ds(layer(e) % 2, 1), (1 - k) * FI:(2 - k) * FI].squeeze(1),
                                      ALU.add).then_inc(hb_set, 1)

                def gate_u(e):
                    wait(dve, gelu_set, e, 1, 1)
                    wait(dve, hb_set, e, 2, 2)
                    dve.tensor_tensor(hu[:, :], ha[:, :], hg[:, :], ALU.mult).then_inc(hu_set, 1)

                def add_y2(e):
                    wait(dve, w2_done, e, 1, 1)
                    wait(dve, y1b_set, e, 1, 1)
                    wait(dve, y_kept, e.back(1), 1, 1)
                    dve.tensor_tensor(y2s[:, :], M[1][:, 0:D], y1b[:, e.u % 2, :], ALU.add).then_inc(y2_set, 1)

                do(at, 4, sum_exp)
                do(at, 4, invert_sum)
                do(at, 2, rope_sin, 0)
                do(at, 2, rope_sin, 1)
                do(at, 7, add_b1, 1)
                do(at, 7, gate_u)
                do(at, 6, norm)
                do(at, 1, sum_squares, 0)
                do(at, 3, row_max, 0)
                do(at, 4, turn_edge)
                do(at, 5, add_y1)
                do(at, 7, add_y2)
                do(at, 1, sum_squares, 1)
                do(at, 4, turn_rest)
                do(at, 3, row_max, 1)
                do(at, 3, subtract_max, 0)
                do(at, 3, subtract_max, 1)
                do(at, 5, stats)
                do(at, 1, rope_cos)
                do(at, 5, mean_var)
                do(at, 6, add_b1, 0)
                do(at, 5, add_eps)

            run(dve, step)
            for b in range(B):
                dve.wait_ge(y_kept, G * UN - (B - 1 - b) * UN)
                xb = x1[:, b * UN:(b + 1) * UN, :].rearrange("p t d -> p (t d)")
                dve.scalar_tensor_tensor(xb, y[:, b * UN:(b + 1) * UN, :].rearrange("p t d -> p (t d)"),
                                         tgate[:, 1:2], xb, ALU.mult, ALU.add).then_inc(x1_set, 1)

        @block.gpsimd
        def _(pool):
            pool.memset(kT[:, 1, :, 0:WIN], 0.0).then_inc(const_set, 1)
            pool.memset(pT[:, :, :], 0.0).then_inc(pT_zero, 1)
            pool.wait_ge(zero_set, 1)
            pool.wait_ge(xs_ve, 1)
            pool.tensor_tensor(rs16[:, :], ve16[:, :], mhalf[:, 0:NT], ALU.pow).then_inc(xs_rstd, 1)
            pool.wait_ge(rope_in, 16 * 5)

            def scale_tables(l):
                for a in range(2):
                    pool.tensor_tensor(tab[:, l, :, a, :], ropeb[:, :, a, :],
                                       qks[:, a, l, :].unsqueeze(1).to_broadcast([P, UN, DH]), ALU.mult)\
                        .then_inc(tab_set, 1)
                    for n in range(2):
                        o = (1 - n) * HALF
                        pool.tensor_tensor(tab[:, l, :, 2 + a, n * HALF:(n + 1) * HALF],
                                           ropeb[:, :, 2 + a, n * HALF:(n + 1) * HALF],
                                           qks[:, a, l, o:o + HALF].unsqueeze(1).to_broadcast([P, UN, HALF]),
                                           ALU.mult).then_inc(tab_set, 1)

            for l in range(L):
                scale_tables(l)
            pool.wait_ge(xs_ve, 2)
            pool.tensor_tensor(rs16[:, :], ve16[:, :], mhalf[:, 0:NT], ALU.pow).then_inc(xs_rstd, 1)

            def step(at):
                def add_parts(n):
                    wait(pool, roped, n, 3, 3)
                    wait(pool, roped_k, n, 1, 1)
                    for k in range(2):
                        pool.tensor_tensor(t1[:, k * INNER:(k + 1) * INNER], t1[:, k * INNER:(k + 1) * INNER],
                                           t2[:, k * INNER:(k + 1) * INNER], ALU.add).then_inc(rope_sum, 1)

                def rope_sin_k(r):
                    pool.wait_ge(tab_set, 6 * L)
                    wait(pool, qk_copied, r, 4, 4)
                    wait(pool, rope_sum, r.back(1), 2, 2)
                    tb = tab[:, bass.ds(layer(r), 1), r.u, 3, HALF:DH]
                    pool.tensor_tensor(t2[:, INNER:2 * INNER].rearrange("p (h d) -> p h d", h=H)[:, :, HALF:DH],
                                       qk[:, r.u % 2, INNER:2 * INNER].rearrange("p (h d) -> p h d", h=H)[:, :, 0:HALF],
                                       tb.to_broadcast([P, H, HALF]), ALU.mult).then_inc(roped_k, 1)

                def over_norm(n):
                    wait(pool, rn_set, n, 1, 1)
                    wait(pool, turned, n.back(1), 4, 4)
                    for k in range(2):
                        wait(pool, rope_sum, n, 2, k + 1)
                        pool.tensor_tensor(qkr[:, k * INNER:(k + 1) * INNER].rearrange("p (a d) -> p a d", d=DH),
                                           t1[:, k * INNER:(k + 1) * INNER].rearrange("p (a d) -> p a d", d=DH),
                                           rn[:, n.u % 2, k * H:(k + 1) * H].unsqueeze(2)
                                           .to_broadcast([P, H, DH]), ALU.mult).then_inc(qkr_set, 1)

                def invert_norms(r):
                    wait(pool, ss_set, r, 3, 3)
                    wait(pool, qkr_set, r.back(2), 2, 2)
                    pool.tensor_tensor(rn[:, r.u % 2, :], ss[:, r.u % 2, :], mhalf[:, :], ALU.pow).then_inc(rn_set, 1)

                def add_b2(f):
                    pool.wait_ge(wrest_in, 16 * NREST)
                    wait(pool, y1_set, f, 1, 1)
                    wait(pool, y2_set, f.back(2), 1, 1)
                    pool.tensor_tensor(y1b[:, f.u % 2, :], y1s[:, :],
                                       b2b[:, bass.ds(layer(f) % 2, 1), :].squeeze(1), ALU.add).then_inc(y1b_set, 1)

                def probabilities(t):
                    wait(pool, rsum_set, t, 1, 1)
                    wait(pool, pT_set, t.back(1), 8, 8)
                    pool.tensor_tensor(ex[:, :, :], ex[:, :, :],
                                       rsum[:, :].unsqueeze(2).to_broadcast([P, H, 2 * WIN]), ALU.mult)\
                        .then_inc(p_set, 1)

                def invert_deviation(f):
                    wait(pool, ve_set, f, 1, 1)
                    wait(pool, xn_set, f.back(1), 1, 1)
                    pool.tensor_tensor(rstd[:, :], ve[:, :], mhalf[:, 0:1], ALU.pow).then_inc(rstd_set, 1)

                do(at, 2, add_parts)
                do(at, 5, add_b2)
                do(at, 2, over_norm)
                do(at, 1, invert_norms)
                do(at, 1, rope_sin_k)
                do(at, 5, invert_deviation)
                do(at, 3, probabilities)

            run(pool, step)


_INS = ["x", "ctx_1024", "g_xattn", "g_ffn", "L0_xattn_Wq", "L0_xattn_bq", "L0_xattn_Wk", "L0_xattn_bk",
        "L0_xattn_Wv", "L0_xattn_bv", "L0_ffn_Wqkv", "L0_ffn_q_scale", "L0_ffn_k_scale", "L0_ffn_Wo",
        "L0_ffn_ln_g", "L0_ffn_ln_b", "L0_ffn_W1", "L0_ffn_b1", "L0_ffn_W2", "L0_ffn_b2"]


def _constants(n, dh):
    import numpy as np

    f = np.float32
    half = np.arange(0, dh, 2, dtype=f)
    inv_freq = (f(1.0) / f(10000.0) ** (half / f(dh))).astype(f)
    t = np.arange(n, dtype=f)
    freqs = (t[:, None] * inv_freq[None, :]).astype(f)
    base = ((half + f(0.4 * dh)) / f(1.4 * dh)).astype(f)
    scale = (base[None, :] ** ((t - n // 2) / f(WIN // 2))[:, None]).astype(f)
    cos, sin = np.cos(freqs), np.sin(freqs)
    inv = f(1.0) / scale
    kinds = [np.concatenate([a * m, b * m], -1) for a, b, m in
             ((cos, cos, scale * f(8.0)), (cos, cos, inv), (-sin, sin, scale * f(8.0)), (-sin, sin, inv))]
    rope = np.stack(kinds, 1).reshape(n // P, P, 4, dh).transpose(1, 0, 2, 3)
    i = (np.arange(P) % WIN)[:, None]
    j = np.arange(WIN)[None, :]
    low = f(-3.0e38)
    own = np.where(j > i, low, f(0))
    before = np.where(j < i, low, f(0))
    first = np.where((np.arange(P) < WIN)[:, None], low, before)
    masks = np.stack([np.concatenate([first, own], 1), np.concatenate([before, own], 1)], 1)
    return [np.ascontiguousarray(a, dtype=f) for a in (rope, masks, np.eye(P))]


def kernel(**inputs):
    import numpy as _np
    import concourse.bacc as _bacc
    from concourse import mybir as _mybir
    from concourse.bass_utils import run_bass_kernel_spmd as _run

    nc = _bacc.Bacc("TRN2", target_bir_lowering=False, num_devices=1)
    arrays, args = {}, []
    named = [(n, inputs[n]) for n in _INS]
    named += list(zip(("rope", "masks", "ident"), _constants(inputs["x"].shape[1], inputs["L0_ffn_q_scale"].shape[1])))
    for name, a in named:
        if name in ("L0_ffn_ln_g", "L0_ffn_ln_b"):
            a = _np.asarray(a).T
        a = _np.ascontiguousarray(a)
        arrays[f"in_{name}_dram"] = a
        args.append(nc.dram_tensor(f"in_{name}_dram", a.shape, _mybir.dt.from_np(a.dtype), kind="ExternalInput").ap())
    args.append(nc.dram_tensor("out_dram", inputs["x"].shape, _mybir.dt.float32, kind="ExternalOutput").ap())
    build(nc, *args)
    return _run(nc, [arrays], core_ids=[0]).results[0]["out_dram"]
```
